# Optimizing a Trainium2 kernel written in Bass

```python
import numpy as np
import jax
import jax.numpy as jnp

def _softmax(x, axis=-1):
    return jax.nn.softmax(x, axis=axis)
def _gelu(x):
    return jax.nn.gelu(x, approximate=True)
def _silu(x):
    return jax.nn.silu(x)
def _sigmoid(x):
    return jax.nn.sigmoid(x)
def _layernorm(x, axis=-1, eps=1e-5):
    m = jnp.mean(x, axis=axis, keepdims=True)
    v = jnp.var(x, axis=axis, keepdims=True)
    return (x - m) / jnp.sqrt(v + eps)
def _scatter_add(tgt, idx, src, axis=0):
    return tgt.at[idx].add(src)
def _segment_sum(src, seg, n):
    return jax.ops.segment_sum(src, seg, n)

kernel_name = 'mk_conv_seq_d4_conv_nhwc768_7300a9'

def setup_inputs(seed: int = 0):
    np.random.seed(seed)
    _w = jnp.asarray
    def _rec_inputs():
        import jax
        import jax.numpy as jnp
        _gk = jax.random.key(seed)
        x = -4.65e-05 + 0.9999 * jax.random.normal(jax.random.fold_in(_gk, 1), (2, 128, 128, 768), jnp.float32)
        return x
    x = _rec_inputs()
    def _L0_conv_setup():
        import jax, jax.numpy as jnp
        import numpy as np
        NUM_BLOCKS = 8
        SPARSITY = 0.01
        HARD_FRAC = 1.0

        def softshrink(x, lam):
            return jnp.sign(x) * jnp.maximum(jnp.abs(x) - lam, 0.0)
        key = jax.random.key(seed)
        ks = jax.random.split(key, 5)
        B, H, W, C = (4, 128, 128, 768)
        nb = NUM_BLOCKS
        bs = C // nb
        scale = 0.02
        return {'x': jax.random.normal(ks[0], (B, H, W, C), dtype=jnp.float32), 'w1': scale * jax.random.normal(ks[1], (2, nb, bs, bs), dtype=jnp.float32), 'b1': scale * jax.random.normal(ks[2], (2, nb, bs), dtype=jnp.float32), 'w2': scale * jax.random.normal(ks[3], (2, nb, bs, bs), dtype=jnp.float32), 'b2': scale * jax.random.normal(ks[4], (2, nb, bs), dtype=jnp.float32)}
    _L0_conv_all = _L0_conv_setup()
    _L0_conv_in = {k: v for k, v in _L0_conv_all.items() if k in ('w1', 'b1', 'w2', 'b2', )}
    del _L0_conv_all

    def _L1_conv_setup():
        import jax, jax.numpy as jnp
        import numpy as np
        NUM_HEADS = 8
        HIDDEN_SIZE = 768
        BLOCK = HIDDEN_SIZE // NUM_HEADS
        FACTOR = 1
        LAMBDA = 0.01
        FRACTION = 1.0
        SCALE = 0.02

        def softshrink(x, lambd):
            return jnp.where(x > lambd, x - lambd, jnp.where(x < -lambd, x + lambd, jnp.zeros_like(x)))
        key = jax.random.key(seed)
        k = jax.random.split(key, 5)
        B, H, W = (4, 128, 128)
        x = jax.random.normal(k[0], (B, H, W, HIDDEN_SIZE), dtype=jnp.float32)
        w1 = SCALE * jax.random.normal(k[1], (2, NUM_HEADS, BLOCK, BLOCK * FACTOR), dtype=jnp.float32)
        b1 = SCALE * jax.random.normal(k[2], (2, NUM_HEADS, BLOCK * FACTOR), dtype=jnp.float32)
        w2 = SCALE * jax.random.normal(k[3], (2, NUM_HEADS, BLOCK * FACTOR, BLOCK), dtype=jnp.float32)
        b2 = SCALE * jax.random.normal(k[4], (2, NUM_HEADS, BLOCK), dtype=jnp.float32)
        return {'x': x, 'w1': w1, 'b1': b1, 'w2': w2, 'b2': b2}
    _L1_conv_all = _L1_conv_setup()
    _L1_conv_in = {k: v for k, v in _L1_conv_all.items() if k in ('w1', 'b1', 'w2', 'b2', )}
    del _L1_conv_all

    def _L2_conv_setup():
        import jax, jax.numpy as jnp
        import numpy as np
        NUM_HEADS = 8
        HIDDEN_SIZE = 768
        BLOCK = HIDDEN_SIZE // NUM_HEADS
        FACTOR = 1
        LAMBDA = 0.01
        FRACTION = 1.0
        SCALE = 0.02

        def softshrink(x, lambd):
            return jnp.where(x > lambd, x - lambd, jnp.where(x < -lambd, x + lambd, jnp.zeros_like(x)))
        key = jax.random.key(seed)
        k = jax.random.split(key, 5)
        B, H, W = (4, 128, 128)
        x = jax.random.normal(k[0], (B, H, W, HIDDEN_SIZE), dtype=jnp.float32)
        w1 = SCALE * jax.random.normal(k[1], (2, NUM_HEADS, BLOCK, BLOCK * FACTOR), dtype=jnp.float32)
        b1 = SCALE * jax.random.normal(k[2], (2, NUM_HEADS, BLOCK * FACTOR), dtype=jnp.float32)
        w2 = SCALE * jax.random.normal(k[3], (2, NUM_HEADS, BLOCK * FACTOR, BLOCK), dtype=jnp.float32)
        b2 = SCALE * jax.random.normal(k[4], (2, NUM_HEADS, BLOCK), dtype=jnp.float32)
        return {'x': x, 'w1': w1, 'b1': b1, 'w2': w2, 'b2': b2}
    _L2_conv_all = _L2_conv_setup()
    _L2_conv_in = {k: v for k, v in _L2_conv_all.items() if k in ('w1', 'b1', 'w2', 'b2', )}
    del _L2_conv_all

    def _L3_conv_setup():
        import jax, jax.numpy as jnp
        import numpy as np
        NUM_BLOCKS = 8
        BLOCK = 96
        FACTOR = 1
        LAM = 0.01
        FRAC = 1.0
        SCALE = 0.02

        def _softshrink(v, lam):
            return jnp.where(v > lam, v - lam, jnp.where(v < -lam, v + lam, 0.0))
        key = jax.random.key(seed)
        k1, k2, k3, k4, k5 = jax.random.split(key, 5)
        B, H, W, C = (4, 90, 180, 768)
        x = jax.random.normal(k1, (B, H, W, C), jnp.float32)
        w1 = SCALE * jax.random.normal(k2, (2, NUM_BLOCKS, BLOCK, BLOCK * FACTOR), jnp.float32)
        b1 = SCALE * jax.random.normal(k3, (2, NUM_BLOCKS, BLOCK * FACTOR), jnp.float32)
        w2 = SCALE * jax.random.normal(k4, (2, NUM_BLOCKS, BLOCK * FACTOR, BLOCK), jnp.float32)
        b2 = SCALE * jax.random.normal(k5, (2, NUM_BLOCKS, BLOCK), jnp.float32)
        return {'x': x, 'w1': w1, 'b1': b1, 'w2': w2, 'b2': b2}
    _L3_conv_all = _L3_conv_setup()
    _L3_conv_in = {k: v for k, v in _L3_conv_all.items() if k in ('w1', 'b1', 'w2', 'b2', )}
    del _L3_conv_all

    return {
        "x": x,
        "L0_conv_w1": _L0_conv_in["w1"],
        "L0_conv_b1": _L0_conv_in["b1"],
        "L0_conv_w2": _L0_conv_in["w2"],
        "L0_conv_b2": _L0_conv_in["b2"],
        "L1_conv_w1": _L1_conv_in["w1"],
        "L1_conv_b1": _L1_conv_in["b1"],
        "L1_conv_w2": _L1_conv_in["w2"],
        "L1_conv_b2": _L1_conv_in["b2"],
        "L2_conv_w1": _L2_conv_in["w1"],
        "L2_conv_b1": _L2_conv_in["b1"],
        "L2_conv_w2": _L2_conv_in["w2"],
        "L2_conv_b2": _L2_conv_in["b2"],
        "L3_conv_w1": _L3_conv_in["w1"],
        "L3_conv_b1": _L3_conv_in["b1"],
        "L3_conv_w2": _L3_conv_in["w2"],
        "L3_conv_b2": _L3_conv_in["b2"],
    }

def reference(x, L0_conv_w1, L0_conv_b1, L0_conv_w2, L0_conv_b2, L1_conv_w1, L1_conv_b1, L1_conv_w2, L1_conv_b2, L2_conv_w1, L2_conv_b1, L2_conv_w2, L2_conv_b2, L3_conv_w1, L3_conv_b1, L3_conv_w2, L3_conv_b2):
    import jax
    import jax.numpy as jnp
    def _L0_conv_ref(x, w1, b1, w2, b2):
        import jax, jax.numpy as jnp
        import numpy as np
        NUM_BLOCKS = 8
        SPARSITY = 0.01
        HARD_FRAC = 1.0

        def softshrink(x, lam):
            return jnp.sign(x) * jnp.maximum(jnp.abs(x) - lam, 0.0)
        bias = x
        dtype = x.dtype
        xf32 = x.astype(jnp.float32)
        B, H, W, C = x.shape
        nb = NUM_BLOCKS
        bs = C // nb
        Wf = W // 2 + 1
        xh = jnp.fft.rfft2(xf32, axes=(1, 2), norm='ortho')
        xh = xh.reshape(B, H, Wf, nb, bs)
        total_modes = H // 2 + 1
        kept_modes = int(total_modes * HARD_FRAC)
        s = total_modes + kept_modes
        d = total_modes - kept_modes
        xk = xh[:, d:s, :kept_modes]
        xr, xi = (xk.real, xk.imag)
        ein = lambda a, w: jnp.einsum('bhfni,nio->bhfno', a, w)
        o1r = jax.nn.relu(ein(xr, w1[0]) - ein(xi, w1[1]) + b1[0])
        o1i = jax.nn.relu(ein(xi, w1[0]) + ein(xr, w1[1]) + b1[1])
        o2r_k = ein(o1r, w2[0]) - ein(o1i, w2[1]) + b2[0]
        o2i_k = ein(o1i, w2[0]) + ein(o1r, w2[1]) + b2[1]
        o2r = jnp.zeros((B, H, Wf, nb, bs), jnp.float32).at[:, d:s, :kept_modes].set(o2r_k)
        o2i = jnp.zeros((B, H, Wf, nb, bs), jnp.float32).at[:, d:s, :kept_modes].set(o2i_k)
        yr = softshrink(o2r, SPARSITY)
        yi = softshrink(o2i, SPARSITY)
        y = (yr + 1j * yi).reshape(B, H, Wf, C)
        out = jnp.fft.irfft2(y, s=(H, W), axes=(1, 2), norm='ortho').astype(dtype)
        return out + bias

    def _L1_conv_ref(x, w1, b1, w2, b2):
        import jax, jax.numpy as jnp
        import numpy as np
        NUM_HEADS = 8
        HIDDEN_SIZE = 768
        BLOCK = HIDDEN_SIZE // NUM_HEADS
        FACTOR = 1
        LAMBDA = 0.01
        FRACTION = 1.0
        SCALE = 0.02

        def softshrink(x, lambd):
            return jnp.where(x > lambd, x - lambd, jnp.where(x < -lambd, x + lambd, jnp.zeros_like(x)))
        bias = x
        dtype = x.dtype
        xf32 = x.astype(jnp.float32)
        B, H, W, C = x.shape
        xs = jnp.fft.rfft2(xf32, axes=(1, 2))
        Wm = W // 2 + 1
        xs = xs.reshape(B, H, Wm, NUM_HEADS, BLOCK)
        total_modes = H // 2 + 1
        kept = int(total_modes * FRACTION)
        lo, hi = (total_modes - kept, min(total_modes + kept, H))
        wk = min(kept, Wm)
        xr = jnp.real(xs[:, lo:hi, :wk])
        xi = jnp.imag(xs[:, lo:hi, :wk])
        o1r = jax.nn.relu(jnp.einsum('bxyhi,hio->bxyho', xr, w1[0]) - jnp.einsum('bxyhi,hio->bxyho', xi, w1[1]) + b1[0])
        o1i = jax.nn.relu(jnp.einsum('bxyhi,hio->bxyho', xi, w1[0]) + jnp.einsum('bxyhi,hio->bxyho', xr, w1[1]) + b1[1])
        o2r = jnp.einsum('bxyho,hoi->bxyhi', o1r, w2[0]) - jnp.einsum('bxyho,hoi->bxyhi', o1i, w2[1]) + b2[0]
        o2i = jnp.einsum('bxyho,hoi->bxyhi', o1i, w2[0]) + jnp.einsum('bxyho,hoi->bxyhi', o1r, w2[1]) + b2[1]
        zr = jnp.zeros((B, H, Wm, NUM_HEADS, BLOCK), dtype=jnp.float32).at[:, lo:hi, :wk].set(o2r)
        zi = jnp.zeros((B, H, Wm, NUM_HEADS, BLOCK), dtype=jnp.float32).at[:, lo:hi, :wk].set(o2i)
        out_c = softshrink(zr, LAMBDA) + 1j * softshrink(zi, LAMBDA)
        out_c = out_c.reshape(B, H, Wm, C)
        out = jnp.fft.irfft2(out_c, s=(H, W), axes=(1, 2))
        return out.astype(dtype) + bias

    def _L2_conv_ref(x, w1, b1, w2, b2):
        import jax, jax.numpy as jnp
        import numpy as np
        NUM_HEADS = 8
        HIDDEN_SIZE = 768
        BLOCK = HIDDEN_SIZE // NUM_HEADS
        FACTOR = 1
        LAMBDA = 0.01
        FRACTION = 1.0
        SCALE = 0.02

        def softshrink(x, lambd):
            return jnp.where(x > lambd, x - lambd, jnp.where(x < -lambd, x + lambd, jnp.zeros_like(x)))
        bias = x
        dtype = x.dtype
        xf32 = x.astype(jnp.float32)
        B, H, W, C = x.shape
        xs = jnp.fft.rfft2(xf32, axes=(1, 2))
        Wm = W // 2 + 1
        xs = xs.reshape(B, H, Wm, NUM_HEADS, BLOCK)
        total_modes = H // 2 + 1
        kept = int(total_modes * FRACTION)
        lo, hi = (total_modes - kept, min(total_modes + kept, H))
        wk = min(kept, Wm)
        xr = jnp.real(xs[:, lo:hi, :wk])
        xi = jnp.imag(xs[:, lo:hi, :wk])
        o1r = jax.nn.relu(jnp.einsum('bxyhi,hio->bxyho', xr, w1[0]) - jnp.einsum('bxyhi,hio->bxyho', xi, w1[1]) + b1[0])
        o1i = jax.nn.relu(jnp.einsum('bxyhi,hio->bxyho', xi, w1[0]) + jnp.einsum('bxyhi,hio->bxyho', xr, w1[1]) + b1[1])
        o2r = jnp.einsum('bxyho,hoi->bxyhi', o1r, w2[0]) - jnp.einsum('bxyho,hoi->bxyhi', o1i, w2[1]) + b2[0]
        o2i = jnp.einsum('bxyho,hoi->bxyhi', o1i, w2[0]) + jnp.einsum('bxyho,hoi->bxyhi', o1r, w2[1]) + b2[1]
        zr = jnp.zeros((B, H, Wm, NUM_HEADS, BLOCK), dtype=jnp.float32).at[:, lo:hi, :wk].set(o2r)
        zi = jnp.zeros((B, H, Wm, NUM_HEADS, BLOCK), dtype=jnp.float32).at[:, lo:hi, :wk].set(o2i)
        out_c = softshrink(zr, LAMBDA) + 1j * softshrink(zi, LAMBDA)
        out_c = out_c.reshape(B, H, Wm, C)
        out = jnp.fft.irfft2(out_c, s=(H, W), axes=(1, 2))
        return out.astype(dtype) + bias

    def _L3_conv_ref(x, w1, b1, w2, b2):
        import jax, jax.numpy as jnp
        import numpy as np
        NUM_BLOCKS = 8
        BLOCK = 96
        FACTOR = 1
        LAM = 0.01
        FRAC = 1.0
        SCALE = 0.02

        def _softshrink(v, lam):
            return jnp.where(v > lam, v - lam, jnp.where(v < -lam, v + lam, 0.0))
        B, H, W, C = x.shape
        xf = x.astype(jnp.float32)
        f = jnp.fft.fft2(xf, axes=(1, 2), norm='ortho')
        Xh = f.real - f.imag
        Wf = W // 2 + 1
        Xh = Xh[:, :, :Wf, :].reshape(B, H, Wf, NUM_BLOCKS, BLOCK)
        total = H // 2 + 1
        kept = int(total * FRAC)
        lo, hi = (total - kept, min(total + kept, H))
        Xk = Xh[:, lo:hi, :kept]
        o1 = jax.nn.relu(jnp.einsum('bhwni,nio->bhwno', Xk, w1[0]) + b1[0])
        o2 = jnp.einsum('bhwni,nio->bhwno', o1, w2[0]) + b2[0]
        spec = jnp.zeros((B, H, Wf, NUM_BLOCKS, BLOCK), jnp.float32)
        spec = spec.at[:, lo:hi, :kept].set(_softshrink(o2, LAM))
        spec = spec.reshape(B, H, Wf, C).astype(jnp.complex64)
        y = jnp.fft.ifft2(spec, s=(H, W), axes=(1, 2), norm='ortho').real
        return y.astype(x.dtype) + x

    def _gn(v, G=32, eps=1e-5):
        B_, H_, W_, C_ = v.shape
        g = v.reshape(B_, H_, W_, G, C_ // G)
        m = jnp.mean(g, axis=(1, 2, 4), keepdims=True)
        s = jnp.var(g, axis=(1, 2, 4), keepdims=True)
        return ((g - m) / jnp.sqrt(s + eps)).reshape(v.shape)

    def _ln_c(v, eps=1e-6):
        m = jnp.mean(v, axis=-1, keepdims=True)
        s = jnp.var(v, axis=-1, keepdims=True)
        return (v - m) / jnp.sqrt(s + eps)

    def _ln_t(v, eps=1e-5):
        m = jnp.mean(v, axis=-1, keepdims=True)
        s = jnp.var(v, axis=-1, keepdims=True)
        return (v - m) / jnp.sqrt(s + eps)

    def _to_tokens(v):
        B_, H_, W_, C_ = v.shape
        return v.reshape(B_, H_ * W_, C_)
    def _from_tokens(t, like):
        return t.reshape(like.shape)

    x = _L0_conv_ref(x, L0_conv_w1, L0_conv_b1, L0_conv_w2, L0_conv_b2)
    x = _L1_conv_ref(x, L1_conv_w1, L1_conv_b1, L1_conv_w2, L1_conv_b2)
    x = _L2_conv_ref(x, L2_conv_w1, L2_conv_b1, L2_conv_w2, L2_conv_b2)
    x = _L3_conv_ref(x, L3_conv_w1, L3_conv_b1, L3_conv_w2, L3_conv_b2)
    return x


_drawn_inputs = setup_inputs


def setup_inputs(seed=0):
    import zlib

    import numpy as np

    out = dict(_drawn_inputs(seed))
    spreads = {}
    factors = {'L0_conv_b1': 8.0,
     'L1_conv_b1': 200.0,
     'L1_conv_b2': 200.0,
     'L2_conv_b1': 200.0,
     'L2_conv_b2': 200.0,
     'L3_conv_w1': 6.272,
     'L3_conv_b1': 8.0,
     'L3_conv_w2': 5.206,
     'L3_conv_b2': 7.11}
    for name, (base, spread) in spreads.items():
        noise = np.random.default_rng([zlib.crc32(name.encode()), seed]).standard_normal(out[name].shape)
        drawn = base * np.exp(spread * noise) if base else spread * noise
        out[name] = jnp.asarray(drawn.astype(out[name].dtype))
    for name, factor in factors.items():
        out[name] = (out[name] * factor).astype(out[name].dtype)
    return out
```

```python
from contextlib import ExitStack

import numpy as np

import concourse.bass as bass
from concourse import mybir

F32 = mybir.dt.float32
ALU = mybir.AluOpType
ACT = mybir.ActivationFunctionType

P = 128
H = W = 128
KW = W // 2 + 1
HALF = H // 2
NSUM = HALF + 1
CB = 96
NBLK = 8
NLAYER = 3
LAMBDA = 0.01
HARTLEY_PAD = 72

CONST_SHAPES = [("dft_w_sum", 128), ("dft_w_diff", 128), ("cas_w_sum", HARTLEY_PAD),
                ("cas_w_diff", HARTLEY_PAD), ("dft_h", 128), ("idft_h", 128), ("idft_w_sum", 128),
                ("idft_w_diff", 128), ("icas_w_sum", 128), ("icas_w_diff", 128),
                ("even_part", 128), ("odd_part", 128)]
CONST_COLS = sum(n for _, n in CONST_SHAPES)

NCHUNK = HALF // 4 + 1
LATE_LO, LATE_HI = 32, 96


def landing(h):
    if h > LATE_HI:
        return h
    return h - LATE_LO if h >= LATE_LO else h + (LATE_HI + 1 - LATE_LO)


LOADS = [[(0, 16), (113, 15)], [(16, 16), (97, 16)],
         [(32, 8), (89, 8)], [(40, 8), (81, 8)], [(48, 8), (73, 8)], [(56, 17)]]
EARLY = 2
LOAD_OF = [0] * 4 + [1] * 4 + [2] * 2 + [3] * 2 + [4] * 2 + [5] * 3

A_JOBS = []
for _k in range(NCHUNK):
    A_JOBS.append((list(range(4 * _k, min(4 * _k + 4, NSUM))), True, _k))
    if _k < NCHUNK - 1:
        A_JOBS.append(([HALF + h for h in range(max(1, 4 * _k), 4 * _k + 4)], False, _k))
A_BANKS = [0, 1, 6, 7]
PAIRS = [(0, HALF)] + [(k, k + 1) for k in range(1, HALF - 1, 2)] + [(HALF - 1,)]
QUADS = [tuple(range(k, min(k + 4, KW))) for k in range(0, KW, 4)]
NC4 = CB // 4
TAIL_AT = 3

N_A, N_P, N_Q = len(A_JOBS), len(PAIRS), len(QUADS)
U_A, U_P, U_C = 4 * N_A, NLAYER * N_P + N_Q, 4 * NC4
U_X = NCHUNK + NLAYER * NC4
STAGES = 4


def constants():
    def cos(a):
        return np.cos(2 * np.pi * (a % 128) / 128)

    def sin(a):
        return np.sin(2 * np.pi * (a % 128) / 128)
    n = np.arange(128)
    k65, k63 = np.arange(65), np.arange(1, 64)
    m = {}
    c_w, s_w = cos(np.outer(n, k65)), sin(np.outer(n, k63))
    m["dft_w_sum"] = np.hstack([c_w, s_w])
    m["dft_w_diff"] = np.hstack([-s_w, c_w])
    kp = np.arange(HARTLEY_PAD)
    m["cas_w_sum"] = cos(np.outer(n, kp)) + sin(np.outer(n, kp))
    m["cas_w_diff"] = cos(np.outer(n, kp)) - sin(np.outer(n, kp))
    c_h = cos(np.outer(k65, n))
    c_h[[0, 64]] *= 0.5
    m["dft_h"] = np.vstack([c_h, sin(np.outer(k63, n))])
    m["idft_h"] = np.hstack([cos(np.outer(n, k65)), sin(np.outer(n, k63))])
    up = np.arange(64)
    d_sum = np.vstack([2 * cos(np.outer(up, n)), -2 * sin(np.outer(up, n))])
    d_sum[0] = 1
    d_sum[64] = cos(64 * n)
    d_diff = np.vstack([-2 * sin(np.outer(up, n)), -2 * cos(np.outer(up, n))])
    d_diff[0] = -1
    d_diff[64] = -cos(64 * n)
    scale = 1.0 / (H * W)
    m["idft_w_sum"] = 2 * scale * d_sum
    m["idft_w_diff"] = 2 * scale * d_diff
    ortho = (H * W) ** -0.5
    i_sum, i_diff = np.zeros((128, 128)), np.zeros((128, 128))
    i_sum[:65] = ortho * cos(np.outer(k65, n))
    i_diff[:65] = -ortho * sin(np.outer(k65, n))
    m["icas_w_sum"], m["icas_w_diff"] = i_sum, i_diff
    flip = np.zeros((128, 128))
    flip[n, -n % 128] = 1
    m["even_part"] = (np.eye(128) + flip) / 2
    m["odd_part"] = (np.eye(128) - flip) / 2
    return np.ascontiguousarray(np.hstack([m[name] for name, _ in CONST_SHAPES]).astype(np.float32))


def layer_scales():
    out = np.zeros((NLAYER, P, 6), np.float32)
    for layer in range(NLAYER):
        f, g = ((H * W) ** -0.5, (H * W) ** 0.5) if layer == 0 else (1.0, 1.0)
        out[layer] = [f, -f, g, -g, LAMBDA * g, -LAMBDA * g]
    return out


def spectral_layers(nc, x, w1, w2, b1, scales, hw1, hw2, hb1, consts, out, n_img, n_blk):
    n_unit = n_img * n_blk
    with ExitStack() as ctx:
        def sb(name, shape):
            return ctx.enter_context(nc.sbuf_tensor(name, shape, F32))

        def sem(name):
            return ctx.enter_context(nc.semaphore(name))

        const = sb("const", [P, CONST_COLS])
        mat, at = {}, 0
        for name, cols in CONST_SHAPES:
            mat[name] = const[:, at:at + cols]
            at += cols
        X = sb("X", [P, P, CB])
        Gt = sb("G", [CB, KW * 2 * P])
        G = Gt[:, :].rearrange("c (k t s) -> c k t s", t=2, s=P)
        HG = Gt[:, 2 * P:2 * P + KW * P].rearrange("c (k s) -> c k s", s=P)
        Zt = sb("Z", [P, CB * P])
        Z = Zt[:, :].rearrange("p (c t k) -> p c t k", t=2, k=HALF)
        Zslots = Zt[:, :].rearrange("p (c s) -> p c s", s=P)
        HZ = Zt[:, 0:CB * KW].rearrange("p (c k) -> p c k", k=KW)
        rows_in = Zt[:, :].rearrange("p (h c) -> p h c", c=CB)
        B = [sb(f"B{i}", [P, 4 * CB]) for i in range(2)]
        O1 = [sb(f"O1_{i}", [CB + 1, 4 * P]) for i in range(2)]
        V = [sb(f"V{i}", [P, 4 * P]) for i in range(2)]
        edge = sb("edge", [P, 2, 2, CB])
        clipped = [sb(f"clipped{i}", [P, 4 * CB]) for i in range(2)]
        stage = [sb(f"stage{i}", [P, 8, CB]) for i in range(STAGES)]
        w1_in = sb("w1_in", [CB, 2, CB])
        w2_in = sb("w2_in", [CB + 1, 2, CB])
        b1_in = sb("b1_in", [CB, 2])
        scale_in = sb("scale_in", [P, 6])
        hw1_in = sb("hw1_in", [CB, CB])
        hw2_in = sb("hw2_in", [CB + 1, CB])
        hb1_in = sb("hb1_in", [CB, 1])
        M1 = sb("M1", [CB, 2, 2, CB])
        M2 = sb("M2", [CB + 1, 2, 2, CB])
        bias1 = sb("bias1", [CB, 2])
        lam = sb("lam", [P, 2])
        HM1 = sb("HM1", [CB, CB])
        HM2 = sb("HM2", [CB + 1, CB])
        hbias1 = sb("hbias1", [CB, 1])
        bank = ctx.enter_context(nc.psum_tensor("bank", [P, 8, 512], F32))

        const_loaded = sem("const_loaded")
        rows_loaded = [sem(f"rows_loaded{g}") for g in range(len(LOADS))]
        weights_loaded = sem("weights_loaded")
        hweights_loaded = sem("hweights_loaded")
        weights_ready = sem("weights_ready")
        zeroed = sem("zeroed")
        x_ready = sem("x_ready")
        final_ready = sem("final_ready")
        a_done, a_taken = sem("a_done"), sem("a_taken")
        mix_done, mix_taken = sem("mix_done"), sem("mix_taken")
        b_done, b_taken = sem("b_done"), sem("b_taken")
        mlp_done, mlp_clipped, z_ready = sem("mlp_done"), sem("mlp_clipped"), sem("z_ready")
        edge_done, edge_taken = sem("edge_done"), sem("edge_taken")
        c_done, v_ready = sem("c_done"), sem("v_ready")
        d_done = sem("d_done")
        staged = sem("staged")
        stored = [sem(f"stored{i}") for i in range(STAGES)]

        block = ctx.enter_context(nc.Block())

        def load_group(eng, g, image, chan):
            for h0, n in LOADS[g]:
                src = x[bass.ds(image, 1), h0:h0 + n, :, bass.ds(chan, CB)]
                eng.dma_start(rows_in[:, landing(h0):landing(h0) + n, :],
                              src.rearrange("a h w c -> w (a h) c")).then_inc(rows_loaded[g], 16)

        def chunk_rows(k):
            if k == NCHUNK - 1:
                return (HALF, 1), None
            if k == 0:
                return (0, 4), (H - 3, 3)
            return (4 * k, 4), (H - 4 * k - 3, 4)

        @block.sync
        def _(sp):
            sp.dma_start(const[:, :], consts).then_inc(const_loaded, 16)
            for g in range(len(LOADS)):
                load_group(sp, g, 0, 0)

            def boundary(u, image, chan, following):
                if following is not None:
                    sp.wait_ge(c_done, u * U_C + NLAYER * NC4)
                    for g in range(EARLY):
                        load_group(sp, g, *following)
                    sp.wait_ge(c_done, u * U_C + U_C)
                    for g in range(EARLY, len(LOADS)):
                        load_group(sp, g, *following)
                for k in range(NCHUNK):
                    sp.wait_ge(staged, u * NCHUNK + (k + 1))
                    at = 0
                    for rows in chunk_rows(k):
                        if rows is None:
                            continue
                        h0, n = rows
                        dst = out[bass.ds(image, 1), h0:h0 + n, :, bass.ds(chan, CB)]
                        sp.dma_start(dst.rearrange("a h w c -> w (a h) c"),
                                     stage[k % STAGES][:, at:at + n, :]).then_inc(stored[k % STAGES], 16)
                        at += 4

            if n_unit > 1:
                with sp.Fori(0, n_unit - 1) as u:
                    image, chan = sp.snap(u % n_img), sp.snap((u // n_img) * CB)
                    nxt = (sp.snap((u + 1) % n_img), sp.snap(((u + 1) // n_img) * CB))
                    boundary(u, image, chan, nxt)
            last = n_unit - 1
            boundary(last, last % n_img, (last // n_img) * CB, None)
            for s in range(STAGES):
                chunks = [k for k in range(NCHUNK) if k % STAGES == s]
                per_unit = sum(16 * sum(r is not None for r in chunk_rows(k)) for k in chunks)
                sp.wait_ge(stored[s], n_unit * per_unit + 1)

        @block.gpsimd
        def _(pool):
            with pool.Fori(0, n_unit) as u:
                block_of = pool.snap(u // n_img)
                with pool.Fori(0, NLAYER) as layer:
                    index = pool.snap(layer * n_blk + block_of)
                    pool.dma_start(w1_in[:, :, :], w1[bass.ds(index, 1)].rearrange("a c t o -> c (a t) o")).then_inc(weights_loaded, 16)
                    pool.dma_start(w2_in[:, :, :], w2[bass.ds(index, 1)].rearrange("a c t o -> c (a t) o")).then_inc(weights_loaded, 16)
                    pool.dma_start(b1_in[:, :], b1[bass.ds(index, 1)].rearrange("a c t -> c (a t)")).then_inc(weights_loaded, 16)
                    pool.dma_start(scale_in[:, :], scales[bass.ds(layer, 1)].rearrange("a p n -> p (a n)")).then_inc(weights_loaded, 16)
                    pool.wait_ge(weights_ready, u * 4 + layer + 1)
                pool.dma_start(hw1_in[:, :], hw1[bass.ds(block_of, 1)].rearrange("a c o -> c (a o)")).then_inc(hweights_loaded, 16)
                pool.dma_start(hw2_in[:, :], hw2[bass.ds(block_of, 1)].rearrange("a c o -> c (a o)")).then_inc(hweights_loaded, 16)
                pool.dma_start(hb1_in[:, :], hb1[bass.ds(block_of, 1)].rearrange("a c o -> c (a o)")).then_inc(hweights_loaded, 16)
                pool.wait_ge(weights_ready, u * 4 + NLAYER + 1)

        @block.tensor
        def _(pe):
            mm = pe.matmul

            def forward_w(x0, a0, hartley):
                for j, (slots, is_sum, k) in enumerate(A_JOBS):
                    if not hartley and is_sum:
                        pe.wait_ge(x_ready, x0 + (k + 1))
                    if j >= len(A_BANKS):
                        pe.wait_ge(a_taken, a0 + (j + 1 - len(A_BANKS)))
                    b = A_BANKS[j % len(A_BANKS)]
                    kind = "sum" if is_sum else "diff"
                    m = mat[f"cas_w_{kind}"] if hartley else mat[f"dft_w_{kind}"]
                    for i, s in enumerate(slots):
                        last = mm(bank[0:CB, b, i * P:i * P + m.shape[1]], X[:, s, :], m,
                                  start=True, stop=True)
                    last.then_inc(a_done, 1)
                pe.wait_ge(a_taken, a0 + N_A)

            def channel_stages(p0, groups, mix, spectrum, mlp, after):
                n = len(groups)
                for i in range(n + 2):
                    if i < n:
                        if i >= 2:
                            pe.wait_ge(mix_taken, p0 + (i - 1))
                        mix(i, groups[i]).then_inc(mix_done, 1)
                    if 1 <= i <= n:
                        j = i - 1
                        pe.wait_ge(mix_taken, p0 + (j + 1))
                        if j >= 2:
                            pe.wait_ge(b_taken, p0 + (j - 1))
                        spectrum(j, groups[j]).then_inc(b_done, 1)
                    if i >= 2:
                        j = i - 2
                        pe.wait_ge(b_taken, p0 + (j + 1))
                        if j >= 2:
                            pe.wait_ge(z_ready, p0 + (j - 1))
                        mlp(j, groups[j]).then_inc(mlp_done, 1)
                        after(j)
                pe.wait_ge(z_ready, p0 + n)

            def inverse(c0, freed, freed0, stationary, m_sum, m_diff, rows):
                for j in range(NC4 + 1):
                    if j < NC4:
                        if j >= 2:
                            pe.wait_ge(v_ready, c0 + (j - 1))
                        for i in range(4):
                            last = mm(bank[0:rows, 2 + j % 2, i * P:(i + 1) * P], stationary(4 * j + i),
                                      mat["idft_h"], start=True, stop=True)
                        last.then_inc(c_done, 1)
                    if j >= 1:
                        g = j - 1
                        pe.wait_ge(v_ready, c0 + (g + 1))
                        if g >= 2:
                            pe.wait_ge(freed, freed0 + (g - 1))
                        v = V[g % 2][0:rows, :].rearrange("p (c s) -> p c s", s=P)
                        o = bank[:, 4 + g % 2, :].rearrange("p (c s) -> p c s", s=P)
                        mm(o[:, :, 0:NSUM], m_sum, v[:, :, 0:NSUM], start=True, stop=True)
                        mm(o[:, :, NSUM:P], m_diff, v[:, :, NSUM:P], start=True, stop=True).then_inc(d_done, 1)

            pe.wait_ge(const_loaded, 16)
            pe.wait_ge(zeroed, 4)
            with pe.Fori(0, n_unit) as u:
                with pe.Fori(0, NLAYER) as layer:
                    x0 = pe.snap(u * U_X + layer * NC4)
                    p0 = pe.snap(u * U_P + layer * N_P)
                    c0 = pe.snap(u * U_C + layer * NC4)
                    forward_w(x0, pe.snap(u * U_A + layer * N_A), False)
                    pe.wait_ge(weights_ready, u * 4 + layer + 1)

                    def mix(i, kws):
                        for q, kw in enumerate(kws):
                            o = bank[:, i % 2, q * 2 * CB:(q + 1) * 2 * CB]
                            mm(o, G[:, kw, 0, :], M1[:, 0, :, :], start=True, stop=False)
                            last = mm(o, G[:, kw, 1, :], M1[:, 1, :, :], start=False, stop=True)
                        return last

                    def spectrum(i, kws):
                        for n in range(2 * len(kws)):
                            last = mm(bank[0:CB, 2 + i % 2, n * P:(n + 1) * P], B[i % 2][:, n * CB:(n + 1) * CB],
                                      mat["dft_h"], start=True, stop=True)
                        return last

                    def mlp(i, kws):
                        for q, kw in enumerate(kws):
                            o = bank[:, 4 + i % 2, q * 2 * CB:(q + 1) * 2 * CB]
                            mm(o, O1[i % 2][:, 2 * q * P:(2 * q + 1) * P], M2[:, 0, :, :], start=True, stop=False)
                            last = mm(o, O1[i % 2][0:CB, (2 * q + 1) * P:(2 * q + 2) * P], M2[0:CB, 1, :, :],
                                      start=False, stop=True)
                        return last

                    def merge_edges(i):
                        if i == TAIL_AT:
                            pe.wait_ge(z_ready, p0 + 1)
                            o = bank[:, 6, 0:2 * CB]
                            mm(o, mat["even_part"], edge[:, 0, :, :], start=True, stop=False)
                            mm(o, mat["odd_part"], edge[:, 1, :, :], start=False, stop=True).then_inc(edge_done, 1)

                    channel_stages(p0, PAIRS, mix, spectrum, mlp, merge_edges)
                    pe.wait_ge(edge_taken, u * NLAYER + layer + 1)
                    inverse(c0, x_ready, x0 + NCHUNK, lambda c: Zslots[:, c, :],
                            mat["idft_w_sum"], mat["idft_w_diff"], P)
                    pe.wait_ge(x_ready, x0 + (NCHUNK + NC4))

                p0 = pe.snap(u * U_P + NLAYER * N_P)
                c0 = pe.snap(u * U_C + NLAYER * NC4)
                forward_w(None, pe.snap(u * U_A + NLAYER * N_A), True)
                pe.wait_ge(weights_ready, u * 4 + NLAYER + 1)

                def hmix(i, kws):
                    for q, kw in enumerate(kws):
                        last = mm(bank[:, i % 2, q * CB:(q + 1) * CB], HG[:, kw, :], HM1[:, :], start=True, stop=True)
                    return last

                def hspectrum(i, kws):
                    for q in range(len(kws)):
                        last = mm(bank[0:CB, 2 + i % 2, q * P:(q + 1) * P], B[i % 2][:, q * CB:(q + 1) * CB],
                                  mat["dft_h"], start=True, stop=True)
                    return last

                def hmlp(i, kws):
                    for q in range(len(kws)):
                        last = mm(bank[:, 4 + i % 2, q * CB:(q + 1) * CB], O1[i % 2][:, q * P:(q + 1) * P], HM2[:, :],
                                  start=True, stop=True)
                    return last

                channel_stages(p0, QUADS, hmix, hspectrum, hmlp, lambda i: None)
                inverse(c0, final_ready, u * NC4, lambda c: HZ[:, c, :],
                        mat["icas_w_sum"][0:KW, :], mat["icas_w_diff"][0:KW, :], KW)

        @block.scalar
        def _(act):
            def take_a(a0, hartley):
                for j, (slots, is_sum, k) in enumerate(A_JOBS):
                    act.wait_ge(a_done, a0 + (j + 1))
                    n = len(slots)
                    ps = bank[0:CB, A_BANKS[j % len(A_BANKS)], 0:n * P].rearrange("c (s k) -> c s k", k=P)
                    s = slice(slots[0], slots[0] + n)
                    if hartley:
                        act.activation(HG[:, :, s].rearrange("c k s -> c s k"), ps[:, :, 0:KW],
                                       ACT.Copy).then_inc(a_taken, 1)
                        continue
                    inner, every = slice(1, HALF), slice(0, KW)
                    k0, k1 = (every, inner) if is_sum else (inner, every)
                    n0 = k0.stop - k0.start
                    act.activation(G[:, k0, 0, s].rearrange("c k s -> c s k"), ps[:, :, 0:n0], ACT.Copy)
                    act.activation(G[:, k1, 1, s].rearrange("c k s -> c s k"), ps[:, :, n0:P],
                                   ACT.Copy).then_inc(a_taken, 1)

            def take_mix(p0, i, cols):
                act.wait_ge(mix_done, p0 + (i + 1))
                if i >= 2:
                    act.wait_ge(b_done, p0 + (i - 1))
                act.activation(B[i % 2][:, 0:cols], bank[:, i % 2, 0:cols], ACT.Copy).then_inc(mix_taken, 1)

            def take_spectrum(p0, i, n, parts, bias):
                act.wait_ge(b_done, p0 + (i + 1))
                if i >= 2:
                    act.wait_ge(mlp_done, p0 + (i - 1))
                cols = n * parts * P
                o = O1[i % 2][0:CB, 0:cols].rearrange("c (q t k) -> c t q k", t=parts, k=P)
                ps = bank[0:CB, 2 + i % 2, 0:cols].rearrange("c (q t k) -> c t q k", t=parts, k=P)
                for t in range(parts):
                    last = act.activation(o[:, t], ps[:, t], ACT.Relu, bias=bias[:, t:t + 1])
                last.then_inc(b_taken, 1)

            def take_c(c0, rows):
                for j in range(NC4):
                    act.wait_ge(c_done, c0 + (j + 1))
                    if j >= 2:
                        act.wait_ge(d_done, c0 + (j - 1))
                    act.activation(V[j % 2][0:rows, :], bank[0:rows, 2 + j % 2, :], ACT.Copy).then_inc(v_ready, 1)

            def take_groups(p0, groups, width, parts, bias):
                for i in range(len(groups) + 1):
                    if i < len(groups):
                        take_mix(p0, i, len(groups[i]) * width)
                    if i >= 1:
                        take_spectrum(p0, i - 1, len(groups[i - 1]), parts, bias)

            with act.Fori(0, n_unit) as u:
                with act.Fori(0, NLAYER) as layer:
                    take_a(act.snap(u * U_A + layer * N_A), False)
                    act.wait_ge(weights_ready, u * 4 + layer + 1)
                    take_groups(act.snap(u * U_P + layer * N_P), PAIRS, 2 * CB, 2, bias1)
                    take_c(act.snap(u * U_C + layer * NC4), P)
                take_a(act.snap(u * U_A + NLAYER * N_A), True)
                act.wait_ge(weights_ready, u * 4 + NLAYER + 1)
                take_groups(act.snap(u * U_P + NLAYER * N_P), QUADS, CB, 1, hbias1)
                take_c(act.snap(u * U_C + NLAYER * NC4), KW)

        @block.vector
        def _(dve):
            dve.memset(G[:, 0:KW:HALF, 0, NSUM:P], 0.0).then_inc(zeroed, 1)
            dve.memset(G[:, 0:KW:HALF, 1, 0:NSUM], 0.0).then_inc(zeroed, 1)
            for i in range(2):
                dve.memset(O1[i][CB:CB + 1, :], 1.0).then_inc(zeroed, 1)
            for i in range(STAGES):
                dve.memset(stage[i][:, :, 0:1], 0.0).then_inc(stored[i], 1)
            def fold(k, u):
                (h0, n), _ = chunk_rows(k)
                if k == LOAD_OF.index(LOAD_OF[k]):
                    g = LOAD_OF[k]
                    dve.wait_ge(rows_loaded[g], (u + 1) * (16 * len(LOADS[g])))
                if n == 1 or k == 0:
                    a = rows_in[:, landing(h0), :]
                    ins = dve.tensor_tensor(X[:, h0, :], a, a, ALU.add)
                    if n == 1:
                        ins.then_inc(x_ready, 1)
                        return
                    h0, n = 1, 3
                a = rows_in[:, landing(h0):landing(h0) + n, :]
                m0 = landing(H - h0 - n + 1)
                assert landing(H - h0) == m0 + n - 1
                b = rows_in[:, m0:m0 + n, :][:, ::-1, :]
                dve.tensor_tensor(X[:, h0:h0 + n, :], a, b, ALU.add)
                dve.tensor_tensor(X[:, HALF + h0:HALF + h0 + n, :], a, b, ALU.subtract).then_inc(x_ready, 1)

            def unfold(k, u):
                st = stage[k % STAGES]
                chunks = [c for c in range(NCHUNK) if c % STAGES == k % STAGES]
                def incs(cs):
                    return sum(16 * sum(r is not None for r in chunk_rows(c)) for c in cs)
                dve.wait_ge(stored[k % STAGES], u * incs(chunks) + (incs([c for c in chunks if c < k]) + 1))
                (h0, n), mirrors = chunk_rows(k)
                if n == 1 or k == 0:
                    last = dve.tensor_copy(st[:, 0, :], X[:, h0, :])
                    if n == 1:
                        last.then_inc(staged, 1)
                        return
                    h0, n = 1, 3
                e, o = X[:, h0:h0 + n, :], X[:, HALF + h0:HALF + h0 + n, :]
                dve.tensor_tensor(st[:, 4 - n:4, :], e, o, ALU.add)
                dve.tensor_tensor(st[:, 4:4 + n, :][:, ::-1, :], e, o, ALU.subtract).then_inc(staged, 1)

            def shrink(i, p0, cols, clip, dst):
                hi, lo = clip
                ps = bank[:, 4 + i % 2, 0:cols]
                dve.wait_ge(mlp_done, p0 + (i + 1))
                if i >= 2:
                    dve.wait_ge(z_ready, p0 + (i - 1))
                cl = clipped[i % 2][:, 0:cols]
                dve.tensor_scalar(cl, ps, hi, lo, ALU.min, ALU.max).then_inc(mlp_clipped, 1)
                dve.wait_ge(mlp_clipped, p0 + (i + 1))
                dst(ps, cl).then_inc(z_ready, 1)

            for k in range(NCHUNK):
                fold(k, 0)
            with dve.Fori(0, n_unit) as u:
                with dve.Fori(0, NLAYER) as layer:
                    x0 = dve.snap(u * U_X + layer * NC4)
                    p0 = dve.snap(u * U_P + layer * N_P)
                    c0 = dve.snap(u * U_C + layer * NC4)
                    it = dve.snap(u * NLAYER + layer)
                    dve.wait_ge(weights_loaded, (it + 1) * 64)
                    f, nf, g, ng = (scale_in[:, n:n + 1] for n in range(4))
                    dve.tensor_scalar(M1[:, 0, :, :], w1_in[:, :, :], f[0:CB], None, ALU.mult)
                    dve.tensor_scalar(M1[:, 1, 0, :], w1_in[:, 1, :], f[0:CB], None, ALU.mult)
                    dve.tensor_scalar(M1[:, 1, 1, :], w1_in[:, 0, :], nf[0:CB], None, ALU.mult)
                    dve.tensor_scalar(M2[:, 0, :, :], w2_in[:, :, :], g[0:CB + 1], None, ALU.mult)
                    dve.tensor_scalar(M2[0:CB, 1, 0, :], w2_in[0:CB, 1, :], ng[0:CB], None, ALU.mult)
                    dve.tensor_scalar(M2[0:CB, 1, 1, :], w2_in[0:CB, 0, :], g[0:CB], None, ALU.mult)
                    dve.tensor_copy(lam[:, :], scale_in[:, 4:6])
                    dve.tensor_copy(bias1[:, :], b1_in[:, :]).then_inc(weights_ready, 1)
                    dve.wait_ge(weights_ready, u * 4 + layer + 1)
                    for i, kws in enumerate(PAIRS):
                        n = len(kws)

                        def to_z(ps, cl):
                            if i == 0:
                                v = "p (k t c) -> p t k c"
                                return dve.tensor_tensor(edge[:, :, :, :], ps.rearrange(v, k=n, t=2),
                                                         cl.rearrange(v, k=n, t=2), ALU.subtract)
                            v = "p (k t c) -> p k t c"
                            return dve.tensor_tensor(Z[:, :, :, kws[0]:kws[0] + n].rearrange("p c t k -> p k t c"),
                                                     ps.rearrange(v, k=n, t=2), cl.rearrange(v, k=n, t=2), ALU.subtract)

                        shrink(i, p0, n * 2 * CB, (lam[:, 0:1], lam[:, 1:2]), to_z)
                        if i == TAIL_AT + 1:
                            dve.wait_ge(edge_done, it + 1)
                            dve.tensor_copy(Z[:, :, :, 0].rearrange("p c t -> p t c"),
                                            bank[:, 6, 0:2 * CB].rearrange("p (t c) -> p t c", t=2)).then_inc(edge_taken, 1)
                    for j in range(NC4):
                        dve.wait_ge(d_done, c0 + (j + 1))
                        xs = X[:, :, 4 * j:4 * j + 4].rearrange("p s c -> p c s")
                        dve.tensor_tensor(xs, bank[:, 4 + j % 2, :].rearrange("p (c s) -> p c s", s=P), xs,
                                          ALU.add).then_inc(x_ready, 1)

                p0 = dve.snap(u * U_P + NLAYER * N_P)
                c0 = dve.snap(u * U_C + NLAYER * NC4)
                dve.wait_ge(hweights_loaded, (u + 1) * 48)
                dve.tensor_scalar(HM1[:, :], hw1_in[:, :], (H * W) ** -0.5, None, ALU.mult)
                dve.tensor_copy(HM2[:, :], hw2_in[:, :])
                dve.tensor_copy(hbias1[:, :], hb1_in[:, :]).then_inc(weights_ready, 1)
                for i, kws in enumerate(QUADS):
                    n = len(kws)

                    def to_hz(ps, cl):
                        v = "p (k c) -> p k c"
                        return dve.tensor_tensor(HZ[:, :, kws[0]:kws[0] + n].rearrange("p c k -> p k c"),
                                                 ps.rearrange(v, k=n), cl.rearrange(v, k=n), ALU.subtract)

                    shrink(i, p0, n * CB, (LAMBDA, -LAMBDA), to_hz)
                for j in range(NC4):
                    dve.wait_ge(d_done, c0 + (j + 1))
                    xs = X[:, :, 4 * j:4 * j + 4].rearrange("p s c -> p c s")
                    dve.scalar_tensor_tensor(xs, xs, 0.5, bank[:, 4 + j % 2, :].rearrange("p (c s) -> p c s", s=P),
                                             ALU.mult, ALU.add).then_inc(final_ready, 1)
                with dve.If(u < n_unit - 1):
                    dve.wait_ge(final_ready, u * NC4 + NC4)
                    for k in range(NCHUNK):
                        unfold(k, u)
                        dve.wait_ge(staged, u * NCHUNK + (k + 1))
                        fold(k, u + 1)
                with dve.Else():
                    dve.wait_ge(final_ready, u * NC4 + NC4)
                    for k in range(NCHUNK):
                        unfold(k, u)


def build(nc, arrays, shape):
    ins = {}
    for name, a in arrays.items():
        ins[name] = nc.dram_tensor(name, a.shape, F32, kind="ExternalInput").ap()
    out = nc.dram_tensor("out", shape, F32, kind="ExternalOutput").ap()
    spectral_layers(nc, ins["x"], ins["w1"], ins["w2"], ins["b1"], ins["scales"], ins["hw1"], ins["hw2"],
                    ins["hb1"], ins["consts"], out, shape[0], shape[3] // CB)


def lay_out(x, ws):
    c = np.ascontiguousarray
    w1 = np.stack([ws[f"L{n}_conv_w1"] for n in range(NLAYER)])
    w2 = np.stack([ws[f"L{n}_conv_w2"] for n in range(NLAYER)])
    b1 = np.stack([ws[f"L{n}_conv_b1"] for n in range(NLAYER)])
    b2 = np.stack([ws[f"L{n}_conv_b2"] for n in range(NLAYER)])
    w2 = np.concatenate([w2, b2[:, :, :, None, :]], axis=3)
    hw2 = np.concatenate([ws["L3_conv_w2"][0], ws["L3_conv_b2"][0][:, None, :]], axis=1)
    n = NLAYER * w1.shape[2]
    return {
        "x": c(x),
        "w1": c(w1.transpose(0, 2, 3, 1, 4)).reshape(n, CB, 2, CB),
        "w2": c(w2.transpose(0, 2, 3, 1, 4)).reshape(n, CB + 1, 2, CB),
        "b1": c(b1.transpose(0, 2, 3, 1)).reshape(n, CB, 2),
        "scales": layer_scales(),
        "hw1": c(ws["L3_conv_w1"][0]),
        "hw2": c(hw2),
        "hb1": c(ws["L3_conv_b1"][0][:, :, None]),
        "consts": constants(),
    }


def kernel(**inputs):
    import concourse.bacc as _bacc
    from concourse.bass_utils import run_bass_kernel_spmd as _run

    ws = {k: np.asarray(v) for k, v in inputs.items() if k != "x"}
    arrays = lay_out(np.asarray(inputs["x"]), ws)
    nc = _bacc.Bacc("TRN2", target_bir_lowering=False, num_devices=1)
    build(nc, arrays, arrays["x"].shape)
    r = _run(nc, [arrays], core_ids=[0])
    return r.results[0]["out"]
```

```python
from contextlib import ExitStack

import numpy as np

import concourse.bass as bass
from concourse import mybir

F32 = mybir.dt.float32
ALU = mybir.AluOpType
ACT = mybir.ActivationFunctionType

P = 128
H = W = 128
KW = W // 2 + 1
HALF = H // 2
NSUM = HALF + 1
CB = 96
NLAYER = 3
LAMBDA = 0.01
ORTHO = float(H * W) ** 0.5
HARTLEY_GAIN = ORTHO / 2

CONST_SHAPES = [("dft_w", 2 * KW), ("dft_h_re", P), ("dft_h_im", P), ("idft_h", P),
                ("idft_w_sum", P), ("idft_w_diff", P), ("identity", CB),
                ("hartley_scale", 1)]
CONST_COLS = sum(n for _, n in CONST_SHAPES)

NCHUNK = HALF // 4 + 1
LOADS = [(0, 16), (112, 16), (16, 16), (96, 16), (32, 32), (64, 32)]
LOAD_OF = [1] * 4 + [3] * 4 + [5] * 9
N_A = CB // 3
N_B = -(-2 * KW // 4)
GROUPS = [(0, 2)] + [(p, min(4, KW - p)) for p in range(2, KW, 4)]
N_G = len(GROUPS)
N_T = P // 4
N_C = CB // 4
POS = np.array([0, HALF] + list(range(1, HALF)))
RING = 3
HIN_RING = 3


def group_of(position):
    return max(g for g, (p, n) in enumerate(GROUPS) if p <= position)


def chunk_rows(k):
    if k == NCHUNK - 1:
        return [(HALF, 1, 0)]
    if k == 0:
        return [(0, 4, 0), (H - 3, 3, 4)]
    return [(4 * k, 4, 0), (H - 4 * k - 3, 4, 4)]


STORES_BEFORE = [16 * sum(len(chunk_rows(i)) for i in range(k % RING, k, RING)) for k in range(NCHUNK)]
STORES = [16 * sum(len(chunk_rows(i)) for i in range(r, NCHUNK, RING)) for r in range(RING)]


def constants():
    def cos(a):
        return np.cos(2 * np.pi * (a % 128) / 128)

    def sin(a):
        return np.sin(2 * np.pi * (a % 128) / 128)
    n = np.arange(128)
    k65, k63 = np.arange(65), np.arange(1, 64)
    m = {}
    m["dft_w"] = np.hstack([cos(np.outer(n, POS)), -sin(np.outer(n, POS))])
    c_h = cos(np.outer(k65, n))
    c_h[[0, 64]] *= 0.5
    s_h = sin(np.outer(k63, n))
    m["dft_h_re"] = np.vstack([c_h, s_h])
    m["dft_h_im"] = np.vstack([c_h, -s_h])
    m["idft_h"] = np.hstack([cos(np.outer(n, k65)), sin(np.outer(n, k63))])
    edge = cos(np.outer(POS[:2], n))
    c_w, s_w = 2 * cos(np.outer(k63, n)), 2 * sin(np.outer(k63, n))
    m["idft_w_sum"] = np.vstack([edge, c_w, -s_w]) / (H * W)
    m["idft_w_diff"] = np.vstack([-edge, -s_w, -c_w]) / (H * W)
    m["identity"] = np.eye(P, CB)
    m["hartley_scale"] = np.full((P, 1), 1 / ORTHO)
    return np.ascontiguousarray(np.hstack([m[name] for name, _ in CONST_SHAPES]).astype(np.float32))


def layer_scales():
    out = np.zeros((NLAYER, P, 6), np.float32)
    for layer in range(NLAYER):
        f, g = (1 / ORTHO, ORTHO) if layer == 0 else (1.0, 1.0)
        out[layer] = [f, -f, g, -g, LAMBDA * g, -LAMBDA * g]
    return out


def spectral_layers(nc, x, w1, w2, b1, scales, hw1, hw2, hb1, consts, out, n_img, n_blk):
    n_unit = n_img * n_blk
    with ExitStack() as ctx:
        def sb(name, shape):
            return ctx.enter_context(nc.sbuf_tensor(name, shape, F32))

        def sem(name):
            return ctx.enter_context(nc.semaphore(name))

        const = sb("const", [P, CONST_COLS])
        mat, at = {}, 0
        for name, cols in CONST_SHAPES:
            mat[name] = const[:, at:at + cols]
            at += cols
        Xt = sb("X", [P, CB * P])
        X = Xt[:, :].rearrange("p (c s) -> p c s", s=P)
        St = sb("S", [P, KW * 2 * P])
        S = St[0:CB, :].rearrange("c (k t s) -> c k t s", t=2, s=P)
        Sflat = St[0:CB, :]
        V = St[:, 0:P * CB].rearrange("p (h c) -> p h c", c=CB)
        Tt = sb("T", [P, KW * 2 * CB])
        T = Tt[:, :].rearrange("p (k t c) -> p k t c", t=2, c=CB)
        ZT = Tt[:, 0:CB * P].rearrange("p (c s) -> p c s", s=P)
        landing = Tt[:, 0:H * CB].rearrange("p (h c) -> p h c", c=CB)
        O1 = [sb(f"O1_{i}", [CB + 1, 2, 4 * P]) for i in range(2)]
        hin = [sb(f"hin{i}", [CB, 4 * P]) for i in range(HIN_RING)]
        edge = sb("edge", [CB, 2, 2, P])
        odd = [sb(f"odd{i}", [P, 4, CB]) for i in range(2)]
        rows_out = [sb(f"rows_out{i}", [P, 8, CB]) for i in range(RING)]
        w1_in = sb("w1_in", [CB, 2, CB])
        w2_in = sb("w2_in", [CB + 1, 2, CB])
        b1_in = sb("b1_in", [CB, 2])
        scale_in = sb("scale_in", [P, 6])
        hw1_in = sb("hw1_in", [CB, CB])
        hw2_in = sb("hw2_in", [CB + 1, CB])
        hb1_in = sb("hb1_in", [CB, 1])
        M1 = sb("M1", [CB, 2, 2, CB])
        M2 = sb("M2", [CB + 1, 2, 2, CB])
        bias1 = sb("bias1", [CB, 2])
        lam = sb("lam", [P, 2])
        HM1 = sb("HM1", [CB, CB])
        HM2 = sb("HM2", [CB + 1, CB])
        hbias1 = sb("hbias1", [CB, 1])
        bank = ctx.enter_context(nc.psum_tensor("bank", [P, 8, 512], F32))

        const_loaded = sem("const_loaded")
        rows_loaded = [sem(f"rows_loaded{g}") for g in range(len(LOADS))]
        weights_loaded, hweights_loaded = sem("weights_loaded"), sem("hweights_loaded")
        w1_ready, w2_ready, hw_ready = sem("w1_ready"), sem("w2_ready"), sem("hw_ready")
        ones_set = sem("ones_set")
        x_ready = sem("x_ready")
        a_done, a_lower, a_taken = sem("a_done"), sem("a_lower"), sem("a_taken")
        b_done, b_taken = sem("b_done"), [sem("b_taken_act"), sem("b_taken_dve")]
        t_done, t_taken = sem("t_done"), [sem("t_taken_act"), sem("t_taken_dve")]
        c_done, c_taken = sem("c_done"), [sem("c_taken_act"), sem("c_taken_dve")]
        hin_ready = sem("hin_ready")
        mix_done, o1_ready = sem("mix_done"), sem("o1_ready")
        mlp_done, z_upper = sem("mlp_done"), sem("z_upper")
        s_updated = sem("s_updated")
        edge_step = sem("edge_step")
        d_done, odd_ready, rows_ready = sem("d_done"), sem("odd_ready"), sem("rows_ready")
        stored = [sem(f"stored{r}") for r in range(RING)]

        def mix_banks(i):
            return [bank[0:CB, 2 * (i % 2) + t, :] for t in range(2)]

        def mlp_banks(i):
            return [bank[0:CB, 4 + 2 * (i % 2) + t, :] for t in range(2)]

        def a_bank(j):
            return bank[:, j % 4, 0:3 * 2 * KW]

        def b_bank(j):
            return bank[0:CB, 4 + j % 4, :]

        def b_cols(j):
            return slice(4 * j * P, min(4 * j + 4, 2 * KW) * P)

        def t_bank(j):
            return bank[:, j % 4, 0:4 * CB]

        def c_bank(j):
            return bank[:, 4 + j % 4, :]

        def d_banks(k):
            return [bank[:, (4, 6, 2)[k % 3] + t, :] for t in range(2)]

        def take_b(copy, j, b0, e):
            cols = b_cols(j)
            copy(Sflat[:, cols], b_bank(j)[:, 0:cols.stop - cols.start]).then_inc(b_taken[e], 1)

        def take_turn(copy, j, e):
            copy(ZT[:, :, 4 * j:4 * j + 4].rearrange("p c s -> p s c"),
                 t_bank(j).rearrange("p (s c) -> p s c", c=CB)).then_inc(t_taken[e], 1)

        def take_c(copy, j, e):
            copy(V[:, :, 4 * j:4 * j + 4].rearrange("p h c -> p c h"),
                 c_bank(j).rearrange("p (c h) -> p c h", h=P)).then_inc(c_taken[e], 1)

        block = ctx.enter_context(nc.Block())

        @block.sync
        def _(sp):
            def load(g, image, chan):
                h0, n = LOADS[g]
                src = x[bass.ds(image, 1), h0:h0 + n, :, bass.ds(chan, CB)]
                sp.dma_start(landing[:, h0:h0 + n, :],
                             src.rearrange("a h w c -> w (a h) c")).then_inc(rows_loaded[g], 16)

            for g in range(len(LOADS)):
                load(g, 0, 0)
            sp.dma_start(const[:, :], consts).then_inc(const_loaded, 16)
            with sp.Fori(0, n_unit) as u:
                image, chan = sp.snap(u % n_img), sp.snap((u // n_img) * CB)
                following = sp.snap((u + 1) % n_unit)
                image1, chan1 = sp.snap(following % n_img), sp.snap((following // n_img) * CB)
                sp.wait_ge(b_done, u * N_B + N_B)
                for g in range(len(LOADS)):
                    load(g, image1, chan1)
                for k in range(NCHUNK):
                    sp.wait_ge(rows_ready, u * NCHUNK + (k + 2))
                    for h0, n, at in chunk_rows(k):
                        dst = out[bass.ds(image, 1), h0:h0 + n, :, bass.ds(chan, CB)]
                        sp.dma_start(dst.rearrange("a h w c -> w (a h) c"),
                                     rows_out[k % RING][:, at:at + n, :]).then_inc(stored[k % RING], 16)
            for r in range(RING):
                sp.wait_ge(stored[r], 1 + n_unit * STORES[r])

        @block.gpsimd
        def _(pool):
            def fold(k, u):
                if k == LOAD_OF.index(LOAD_OF[k]):
                    for g in (LOAD_OF[k] - 1, LOAD_OF[k]):
                        pool.wait_ge(rows_loaded[g], (u + 1) * 16)
                h0, n = 4 * k, min(4, NSUM - 4 * k)
                if n == 1 or k == 0:
                    a = landing[:, h0, :]
                    ins = pool.tensor_tensor(X[:, :, h0], a, a, ALU.add)
                    if n == 1:
                        ins.then_inc(x_ready, 1)
                        return
                    h0, n = 1, 3
                a = landing[:, h0:h0 + n, :]
                b = landing[:, H - h0 - n + 1:H - h0 + 1, :][:, ::-1, :]
                pool.tensor_tensor(X[:, :, h0:h0 + n].rearrange("p c s -> p s c"), a, b, ALU.add)
                pool.tensor_tensor(X[:, :, HALF + h0:HALF + h0 + n].rearrange("p c s -> p s c"), a, b,
                                   ALU.subtract).then_inc(x_ready, 1)

            for k in range(NCHUNK):
                fold(k, 0)
            pool.wait_ge(const_loaded, 16)
            with pool.Fori(0, n_unit) as u:
                block_of = pool.snap(u // n_img)
                for layer in range(NLAYER):
                    it = u * NLAYER + layer
                    g0 = (u * (NLAYER + 1) + layer) * N_G
                    index = pool.snap(layer * n_blk + block_of)
                    pool.dma_start(w1_in[:, :, :], w1[bass.ds(index, 1)].rearrange("a c t o -> c (a t) o")).then_inc(weights_loaded, 16)
                    pool.dma_start(w2_in[:, :, :], w2[bass.ds(index, 1)].rearrange("a c t o -> c (a t) o")).then_inc(weights_loaded, 16)
                    pool.dma_start(b1_in[:, :], b1[bass.ds(index, 1)].rearrange("a c t -> c (a t)")).then_inc(weights_loaded, 16)
                    pool.dma_start(scale_in[:, :], scales[layer]).then_inc(weights_loaded, 16)
                    pool.wait_ge(weights_loaded, (it + 1) * 64)
                    if layer:
                        pool.wait_ge(mix_done, g0)
                    f, nf, g, ng = (scale_in[:, n:n + 1] for n in range(4))
                    pool.tensor_tensor(M1[:, 0, :, :].rearrange("c t o -> c (t o)"), w1_in[:, :, :].rearrange("c t o -> c (t o)"),
                                       f[0:CB].to_broadcast([CB, 2 * CB]), ALU.mult)
                    pool.tensor_scalar(M1[:, 1, 0, :], w1_in[:, 1, :], nf[0:CB], None, ALU.mult)
                    pool.tensor_scalar(M1[:, 1, 1, :], w1_in[:, 0, :], f[0:CB], None, ALU.mult).then_inc(w1_ready, 1)
                    if layer:
                        pool.wait_ge(s_updated, g0 + 1)
                    pool.tensor_tensor(M2[:, 0, :, :].rearrange("c t o -> c (t o)"), w2_in[:, :, :].rearrange("c t o -> c (t o)"),
                                       g[0:CB + 1].to_broadcast([CB + 1, 2 * CB]), ALU.mult)
                    pool.tensor_copy(bias1[:, :], b1_in[:, :])
                    pool.tensor_copy(lam[:, :], scale_in[:, 4:6])
                    pool.tensor_scalar(M2[0:CB, 1, 0, :], w2_in[0:CB, 1, :], ng[0:CB], None, ALU.mult)
                    pool.tensor_scalar(M2[0:CB, 1, 1, :], w2_in[0:CB, 0, :], g[0:CB], None, ALU.mult).then_inc(w2_ready, 1)
                    if layer == 0:
                        pool.wait_ge(a_done, u * N_A + N_A)
                    for k in range(layer * NCHUNK // NLAYER, (layer + 1) * NCHUNK // NLAYER):
                        fold(k, u + 1)
                    pool.wait_ge(w2_ready, it + 1)
                pool.dma_start(hw1_in[:, :], hw1[bass.ds(block_of, 1)].rearrange("a c o -> c (a o)")).then_inc(hweights_loaded, 16)
                pool.dma_start(hw2_in[:, :], hw2[bass.ds(block_of, 1)].rearrange("a c o -> c (a o)")).then_inc(hweights_loaded, 16)
                pool.dma_start(hb1_in[:, :], hb1[bass.ds(block_of, 1)].rearrange("a c o -> c (a o)")).then_inc(hweights_loaded, 16)
                pool.wait_ge(hweights_loaded, (u + 1) * 48)
                pool.tensor_tensor(HM1[:, :], hw1_in[:, :], mat["hartley_scale"][0:CB].to_broadcast([CB, CB]), ALU.mult)
                pool.tensor_copy(hbias1[:, :], hb1_in[:, :])
                pool.tensor_scalar(HM2[:, :], hw2_in[:, :], HARTLEY_GAIN, None, ALU.mult).then_inc(hw_ready, 1)
                g0 = (u * (NLAYER + 1) + NLAYER) * N_G
                for i, (p0, n) in enumerate(GROUPS):
                    pool.wait_ge(s_updated, g0 + (i + 2 - N_G))
                    if i >= HIN_RING:
                        pool.wait_ge(mix_done, g0 + (i + 1 - HIN_RING))
                    pool.tensor_tensor(hin[i % HIN_RING][:, 0:n * P].rearrange("c (k s) -> c k s", s=P),
                                       S[:, p0:p0 + n, 0, :], S[:, p0:p0 + n, 1, :],
                                       ALU.subtract).then_inc(hin_ready, 1)
                pool.wait_ge(hw_ready, u + 1)
                pool.wait_ge(mlp_done, g0 + N_G)

        @block.tensor
        def _(pe):
            mm = pe.matmul

            def forward(u):
                pe.wait_ge(x_ready, (u + 1) * NCHUNK)
                for j in range(N_A):
                    if j >= 4:
                        pe.wait_ge(a_taken, u * N_A + (j - 3))
                    for i in range(3):
                        last = mm(a_bank(j)[:, i * 2 * KW:(i + 1) * 2 * KW], X[:, 3 * j + i, :], mat["dft_w"],
                                  start=True, stop=True)
                    last.then_inc(a_done, 1)
                    if j == 1:
                        pe.wait_ge(rows_ready, u * NCHUNK + 1)
                pe.wait_ge(a_taken, u * N_A + N_A)
                for j in range(N_B):
                    if j >= 4:
                        pe.wait_ge(b_taken[j % 2], u * len(range(j % 2, N_B, 2)) + ((j - 4) // 2 + 1))
                    for q in range(4 * j, min(4 * j + 4, 2 * KW)):
                        i = q - 4 * j
                        last = mm(b_bank(j)[:, i * P:(i + 1) * P], T[:, q // 2, q % 2, :],
                                  mat[("dft_h_re", "dft_h_im")[q % 2]], start=True, stop=True)
                    last.then_inc(b_done, 1)

            def layer_groups(g0, mix, mlp, before_mlp):
                for i in range(N_G + 1):
                    if i < N_G:
                        mix(i, *GROUPS[i]).then_inc(mix_done, 1)
                    if i >= 1:
                        j = i - 1
                        if j == 0:
                            before_mlp()
                        pe.wait_ge(o1_ready, g0 + (j + 1))
                        pe.wait_ge(s_updated, g0 + (1 if j < 2 else j))
                        mlp(j, *GROUPS[j]).then_inc(mlp_done, 1)

            def inverse(u, s0):
                for j in range(N_T):
                    slots = range(4 * j, 4 * j + 4)
                    pe.wait_ge(s_updated, s0 + (2 + max(group_of(s if s < KW else s - KW + 2) for s in slots)))
                    if j >= 4:
                        pe.wait_ge(t_taken[j % 2], u * (N_T // 2) + ((j - 4) // 2 + 1))
                    for i, s in enumerate(slots):
                        o = t_bank(j)[:, i * CB:(i + 1) * CB]
                        pos, part = (s, 0) if s < KW else (s - KW + 2, 1)
                        last = mm(o, S[:, pos, part, :], mat["identity"][0:CB, :], start=True, stop=s >= 2)
                        if s < 2:
                            last = mm(o, S[:, pos, 1, :], mat["identity"][0:CB, :], start=False, stop=True)
                    last.then_inc(t_done, 1)
                for e in range(2):
                    pe.wait_ge(t_taken[e], (u + 1) * (N_T // 2))
                for j in range(N_C):
                    if j >= 4:
                        pe.wait_ge(c_taken[j % 2], u * (N_C // 2) + ((j - 4) // 2 + 1))
                    for i in range(4):
                        last = mm(c_bank(j)[:, i * P:(i + 1) * P], ZT[:, 4 * j + i, :], mat["idft_h"],
                                  start=True, stop=True)
                    last.then_inc(c_done, 1)
                for e in range(2):
                    pe.wait_ge(c_taken[e], (u + 1) * (N_C // 2))
                for k in range(NCHUNK):
                    if k >= 3:
                        pe.wait_ge(rows_ready, u * NCHUNK + (k - 1))
                    even, odds = d_banks(k)
                    h0, n = 4 * k, min(4, NSUM - 4 * k)
                    s = 1 if n == 1 or k == 0 else 0
                    if n > s:
                        mm(odds[:, s * CB:n * CB], mat["idft_w_diff"], V[:, HALF + h0 + s:HALF + h0 + n, :],
                           start=True, stop=True)
                    mm(even[:, 0:n * CB], mat["idft_w_sum"], V[:, h0:h0 + n, :], start=True,
                       stop=True).then_inc(d_done, 1)

            pe.wait_ge(const_loaded, 16)
            with pe.Fori(0, n_unit) as u:
                forward(u)
                with pe.Fori(0, NLAYER) as layer:
                    it = pe.snap(u * NLAYER + layer + 1)
                    g0 = pe.snap((u * (NLAYER + 1) + layer) * N_G)
                    for e in range(2):
                        pe.wait_ge(b_taken[e], (u + 1) * len(range(e, N_B, 2)))
                    pe.wait_ge(w1_ready, it)

                    def mix(i, p0, n):
                        for t in range(2):
                            o = mix_banks(i)[t][:, 0:n * P].rearrange("c (k s) -> c k s", s=P)
                            for part in range(2):
                                last = mm(o, M1[:, part, t, :], S[:, p0:p0 + n, part, :], start=part == 0, stop=part == 1)
                        return last

                    def mlp(i, p0, n):
                        for t in range(2):
                            o = mlp_banks(i)[t][:, 0:n * P]
                            mm(o, M2[:, 0, t, :], O1[i % 2][:, 0, 0:n * P], start=True, stop=False)
                            last = mm(o, M2[0:CB, 1, t, :], O1[i % 2][0:CB, 1, 0:n * P], start=False, stop=True)
                        return last

                    layer_groups(g0, mix, mlp, lambda: pe.wait_ge(w2_ready, it))

                g0 = pe.snap((u * (NLAYER + 1) + NLAYER) * N_G)
                pe.wait_ge(hw_ready, u + 1)

                def hmix(i, p0, n):
                    pe.wait_ge(hin_ready, u * N_G + (i + 1))
                    return mm(mix_banks(i)[0][:, 0:n * P], HM1[:, :], hin[i % HIN_RING][:, 0:n * P],
                              start=True, stop=True)

                def hmlp(i, p0, n):
                    return mm(mlp_banks(i)[0][:, 0:n * P], HM2[:, :], O1[i % 2][:, 0, 0:n * P], start=True, stop=True)

                layer_groups(g0, hmix, hmlp, lambda: None)
                inverse(u, g0)

        @block.scalar
        def _(act):
            def copy(o, i):
                return act.activation(o, i, ACT.Copy)

            def relu_groups(g0, parts, bias):
                for i, (p0, n) in enumerate(GROUPS):
                    act.wait_ge(mix_done, g0 + (i + 1))
                    if i >= 2:
                        act.wait_ge(mlp_done, g0 + (i - 1))
                    for t in range(parts):
                        last = act.activation(O1[i % 2][0:CB, t, 0:n * P], mix_banks(i)[t][:, 0:n * P], ACT.Relu,
                                              bias=bias[:, t:t + 1])
                    last.then_inc(o1_ready, 1)

            with act.Fori(0, n_unit) as u:
                for j in range(N_A):
                    act.wait_ge(a_lower, u * N_A + (j + 1))
                    copy(T[0:NSUM, :, :, 3 * j:3 * j + 3].rearrange("p k t c -> p c t k"),
                         a_bank(j)[0:NSUM].rearrange("p (c t k) -> p c t k", t=2, k=KW)).then_inc(a_taken, 1)
                for j in range(0, N_B, 2):
                    act.wait_ge(b_done, u * N_B + (j + 1))
                    take_b(copy, j, None, 0)
                with act.Fori(0, NLAYER) as layer:
                    act.wait_ge(w2_ready, u * NLAYER + layer + 1)
                    relu_groups(act.snap((u * (NLAYER + 1) + layer) * N_G), 2, bias1)
                act.wait_ge(hw_ready, u + 1)
                relu_groups(act.snap((u * (NLAYER + 1) + NLAYER) * N_G), 1, hbias1)
                act.wait_ge(x_ready, (u + 2) * NCHUNK)
                for j in range(0, N_T, 2):
                    act.wait_ge(t_done, u * N_T + (j + 1))
                    take_turn(copy, j, 0)
                for j in range(0, N_C, 2):
                    act.wait_ge(c_done, u * N_C + (j + 1))
                    take_c(copy, j, 0)
                for k in range(NCHUNK - 1):
                    act.wait_ge(d_done, u * NCHUNK + (k + 1))
                    if k >= 2:
                        act.wait_ge(rows_ready, u * NCHUNK + k)
                    s = 1 if k == 0 else 0
                    copy(odd[k % 2][:, s:4, :], d_banks(k)[1][:, s * CB:4 * CB].rearrange("p (h c) -> p h c", c=CB)).then_inc(odd_ready, 1)

        @block.vector
        def _(dve):
            for i in range(2):
                dve.memset(O1[i][CB:CB + 1, :, :], 1.0).then_inc(ones_set, 1)
            dve.wait_ge(ones_set, 2)
            dve.memset(edge[:, 0, :, :], 0.0).then_inc(s_updated, 1)
            dve.memset(edge[:, 1, :, :], 0.0).then_inc(rows_ready, 1)
            for r in range(RING):
                dve.memset(rows_out[r][:, :, :], 0.0).then_inc(stored[r], 1)

            def add_shrunk(i, g0, p0, n, parts, hi, lo):
                for op, limit, signal in ((ALU.max, hi, z_upper), (ALU.min, lo, s_updated)):
                    for t in range(parts):
                        s = S[:, p0:p0 + n, t, :]
                        last = dve.scalar_tensor_tensor(s, mlp_banks(i)[t][:, 0:n * P].rearrange("c (k s) -> c k s", s=P),
                                                        limit, s, op, ALU.add)
                    last.then_inc(signal, 1)
                    if signal is z_upper:
                        dve.wait_ge(z_upper, g0 + (i + 1))

            def add_edges(g0, e0, parts, hi, lo, factor):
                y = [mlp_banks(0)[t][:, 0:2 * P].rearrange("c (k s) -> c k s", s=P) for t in range(parts)]
                for t in range(parts):
                    last = dve.tensor_scalar(edge[:, t], y[t], hi, None, ALU.max)
                last.then_inc(edge_step, 1)
                dve.wait_ge(edge_step, e0 + 1)
                for t in range(parts):
                    last = dve.scalar_tensor_tensor(edge[:, t], y[t], lo, edge[:, t], ALU.min, ALU.add)
                last.then_inc(edge_step, 1)
                dve.wait_ge(edge_step, e0 + 2)
                for t in range(parts):
                    s = S[:, 0:2, t, :]
                    last = dve.scalar_tensor_tensor(s, edge[:, t], factor, s, ALU.mult, ALU.add)
                last.then_inc(edge_step, 1)
                dve.wait_ge(edge_step, e0 + 3)
                for t in range(parts):
                    f = factor if t == 0 else -factor
                    s = S[:, 0:2, t, :]
                    dve.scalar_tensor_tensor(s[:, :, 0:1], edge[:, t, :, 0:1], f, s[:, :, 0:1], ALU.mult, ALU.add)
                    last = dve.scalar_tensor_tensor(s[:, :, 1:P], edge[:, t, :, 1:P][:, :, ::-1], f, s[:, :, 1:P],
                                                    ALU.mult, ALU.add)
                last.then_inc(z_upper, 1)
                dve.wait_ge(z_upper, g0 + 1)
                dve.memset(edge[:, 0, 0, 0:1], 0.0).then_inc(s_updated, 1)

            def update_groups(g0, e0, parts, hi, lo, factor):
                for i, (p0, n) in enumerate(GROUPS):
                    dve.wait_ge(mlp_done, g0 + (i + 1))
                    if i == 0:
                        add_edges(g0, e0, parts, hi, lo, factor)
                    else:
                        add_shrunk(i, g0, p0, n, parts, hi, lo)

            with dve.Fori(0, n_unit) as u:
                for j in range(N_A):
                    dve.wait_ge(a_done, u * N_A + (j + 1))
                    dve.tensor_copy(T[HALF:P, :, :, 3 * j:3 * j + 3].rearrange("p k t c -> p c t k"),
                                    a_bank(j)[HALF:P].rearrange("p (c t k) -> p c t k", t=2, k=KW)[:, :, ::-1, :]).then_inc(a_lower, 1)
                for j in range(1, N_B, 2):
                    dve.wait_ge(b_done, u * N_B + (j + 1))
                    take_b(dve.tensor_copy, j, None, 1)
                with dve.Fori(0, NLAYER) as layer:
                    it = dve.snap(u * (NLAYER + 1) + layer)
                    dve.wait_ge(w2_ready, u * NLAYER + layer + 1)
                    update_groups(dve.snap(it * N_G), dve.snap(it * 3), 2, lam[0:CB, 0:1], lam[0:CB, 1:2], 0.5)
                it = u * (NLAYER + 1) + NLAYER
                update_groups(dve.snap(it * N_G), dve.snap(it * 3), 1, LAMBDA * HARTLEY_GAIN,
                              -LAMBDA * HARTLEY_GAIN, 1.0)
                dve.wait_ge(x_ready, (u + 2) * NCHUNK)
                for j in range(1, N_T, 2):
                    dve.wait_ge(t_done, u * N_T + (j + 1))
                    take_turn(dve.tensor_copy, j, 1)
                for j in range(1, N_C, 2):
                    dve.wait_ge(c_done, u * N_C + (j + 1))
                    take_c(dve.tensor_copy, j, 1)
                for k in range(NCHUNK):
                    if k < NCHUNK - 1:
                        dve.wait_ge(odd_ready, u * (NCHUNK - 1) + (k + 1))
                    else:
                        dve.wait_ge(d_done, u * NCHUNK + NCHUNK)
                    dve.wait_ge(stored[k % RING], u * STORES[k % RING] + (1 + STORES_BEFORE[k]))
                    n = min(4, NSUM - 4 * k)
                    s = 1 if n == 1 or k == 0 else 0
                    even = d_banks(k)[0][:, 0:n * CB].rearrange("p (h c) -> p h c", c=CB)
                    o = rows_out[k % RING]
                    if s:
                        last = dve.tensor_copy(o[:, 0, :], even[:, 0, :])
                    if n > s:
                        dve.tensor_tensor(o[:, s:n, :], even[:, s:n, :], odd[k % 2][:, s:n, :], ALU.add)
                        last = dve.tensor_tensor(o[:, 4:4 + n - s, :][:, ::-1, :], even[:, s:n, :], odd[k % 2][:, s:n, :],
                                                 ALU.subtract)
                    last.then_inc(rows_ready, 1)


def build(nc, arrays, shape):
    ins = {}
    for name, a in arrays.items():
        ins[name] = nc.dram_tensor(name, a.shape, F32, kind="ExternalInput").ap()
    out = nc.dram_tensor("out", shape, F32, kind="ExternalOutput").ap()
    spectral_layers(nc, ins["x"], ins["w1"], ins["w2"], ins["b1"], ins["scales"], ins["hw1"], ins["hw2"],
                    ins["hb1"], ins["consts"], out, shape[0], shape[3] // CB)


def lay_out(x, ws):
    c = np.ascontiguousarray
    w1 = np.stack([ws[f"L{n}_conv_w1"] for n in range(NLAYER)])
    w2 = np.stack([ws[f"L{n}_conv_w2"] for n in range(NLAYER)])
    b1 = np.stack([ws[f"L{n}_conv_b1"] for n in range(NLAYER)])
    b2 = np.stack([ws[f"L{n}_conv_b2"] for n in range(NLAYER)])
    w2 = np.concatenate([w2, b2[:, :, :, None, :]], axis=3)
    hw2 = np.concatenate([ws["L3_conv_w2"][0], ws["L3_conv_b2"][0][:, None, :]], axis=1)
    n = NLAYER * w1.shape[2]
    return {
        "x": c(x),
        "w1": c(w1.transpose(0, 2, 3, 1, 4)).reshape(n, CB, 2, CB),
        "w2": c(w2.transpose(0, 2, 3, 1, 4)).reshape(n, CB + 1, 2, CB),
        "b1": c(b1.transpose(0, 2, 3, 1)).reshape(n, CB, 2),
        "scales": layer_scales(),
        "hw1": c(ws["L3_conv_w1"][0]),
        "hw2": c(hw2),
        "hb1": c(ws["L3_conv_b1"][0][:, :, None]),
        "consts": constants(),
    }


def kernel(**inputs):
    import concourse.bacc as _bacc
    from concourse.bass_utils import run_bass_kernel_spmd as _run

    ws = {k: np.asarray(v) for k, v in inputs.items() if k != "x"}
    arrays = lay_out(np.asarray(inputs["x"]), ws)
    nc = _bacc.Bacc("TRN2", target_bir_lowering=False, num_devices=1)
    build(nc, arrays, arrays["x"].shape)
    r = _run(nc, [arrays], core_ids=[0])
    return r.results[0]["out"]
```

```python
from contextlib import ExitStack

import numpy as np

import concourse.bass as bass
from concourse import mybir

F32 = mybir.dt.float32
ALU = mybir.AluOpType
ACT = mybir.ActivationFunctionType

P = 128
H = W = 128
KW = W // 2 + 1
HALF = H // 2
NSUM = HALF + 1
CB = 96
NLAYER = 3
LAMBDA = 0.01
ORTHO = float(H * W) ** 0.5
HARTLEY_GAIN = ORTHO / 2

CONST_SHAPES = [("dft_w", 2 * KW), ("dft_h_re", P), ("dft_h_im", P), ("idft_h", P),
                ("idft_w_sum", P), ("idft_w_diff", P), ("identity", CB),
                ("hartley_scale", 1)]
CONST_COLS = sum(n for _, n in CONST_SHAPES)

NCHUNK = HALF // 4 + 1
LOADS = [(0, 16), (112, 16), (16, 16), (96, 16), (32, 32), (64, 32)]
LOAD_OF = [1] * 4 + [3] * 4 + [5] * 9
N_A = CB // 3
N_B = -(-2 * KW // 4)
GROUPS = [(p, min(4, KW - p)) for p in range(2, KW, 4)]
EDGES = len(GROUPS) // 2
GROUPS[EDGES:EDGES] = [GROUPS.pop(), (0, 2)]
EDGES = GROUPS.index((0, 2))
N_G = len(GROUPS)
N_COMPLEX = NLAYER * N_G
N_STEP = (NLAYER + 1) * N_G
N_T = P // 4
N_C = CB // 4
POS = np.array([0, HALF] + list(range(1, HALF)))
RING = 8
COMB_RING = 3
PREPARE_AT = (3, 5, 11, 13)


def group_of(position):
    return next(g for g, (p, n) in enumerate(GROUPS) if p <= position < p + n)


def product(s, t=0):
    return 3 * min(s, N_COMPLEX) + max(0, s - N_COMPLEX) + t


def step_before(s, t):
    n = product(s, t) - 4
    return None if n < 0 else next(b for b in range(s, -1, -1) if product(b) <= n)


def plain(s):
    return sum(b % N_G != EDGES for b in range(s + 1))


def b_groups(position, e):
    return len(range(e, position // 2 + 1, 2))


def chunk_rows(k):
    if k == NCHUNK - 1:
        return [(HALF, 1, 0)]
    if k == 0:
        return [(0, 4, 0), (H - 3, 3, 4)]
    return [(4 * k, 4, 0), (H - 4 * k - 3, 4, 4)]


STORES_BEFORE = [16 * sum(len(chunk_rows(i)) for i in range(k % RING, k, RING)) for k in range(NCHUNK)]
STORES = [16 * sum(len(chunk_rows(i)) for i in range(r, NCHUNK, RING)) for r in range(RING)]


def constants():
    def cos(a):
        return np.cos(2 * np.pi * (a % 128) / 128)

    def sin(a):
        return np.sin(2 * np.pi * (a % 128) / 128)
    n = np.arange(128)
    k65, k63 = np.arange(65), np.arange(1, 64)
    m = {}
    m["dft_w"] = np.hstack([cos(np.outer(n, POS)), -sin(np.outer(n, POS))])
    c_h = cos(np.outer(k65, n))
    c_h[[0, 64]] *= 0.5
    s_h = sin(np.outer(k63, n))
    m["dft_h_re"] = np.vstack([c_h, s_h])
    m["dft_h_im"] = np.vstack([c_h, -s_h])
    m["idft_h"] = np.hstack([cos(np.outer(n, k65)), sin(np.outer(n, k63))])
    edge = cos(np.outer(POS[:2], n))
    c_w, s_w = 2 * cos(np.outer(k63, n)), 2 * sin(np.outer(k63, n))
    m["idft_w_sum"] = np.vstack([edge, c_w, -s_w]) / (H * W)
    m["idft_w_diff"] = np.vstack([-edge, -s_w, -c_w]) / (H * W)
    m["identity"] = np.eye(P, CB)
    m["hartley_scale"] = np.full((P, 1), 1 / ORTHO)
    return np.ascontiguousarray(np.hstack([m[name] for name, _ in CONST_SHAPES]).astype(np.float32))


def layer_scales():
    out = np.zeros((NLAYER, P, 6), np.float32)
    for layer in range(NLAYER):
        f, g = (1 / ORTHO, ORTHO) if layer == 0 else (1.0, 1.0)
        out[layer] = [f, -f, g, -g, LAMBDA * g, -LAMBDA * g]
        out[layer, CB, 3] = g
    return out


def spectral_layers(nc, x, w1, w2, b1, b2, scales, hw1, hw2, hb1, consts, out, n_img, n_blk):
    n_unit = n_img * n_blk
    with ExitStack() as ctx:
        def sb(name, shape):
            return ctx.enter_context(nc.sbuf_tensor(name, shape, F32))

        def sem(name):
            return ctx.enter_context(nc.semaphore(name))

        const = sb("const", [P, CONST_COLS])
        mat, at = {}, 0
        for name, cols in CONST_SHAPES:
            mat[name] = const[:, at:at + cols]
            at += cols
        Xt = sb("X", [P, CB * P])
        X = Xt[:, :].rearrange("p (c s) -> p c s", s=P)
        St = sb("S", [P, KW * 2 * P])
        S = St[0:CB, :].rearrange("c (k t s) -> c k t s", t=2, s=P)
        Sflat = St[0:CB, :]
        V = St[:, 0:P * CB].rearrange("p (h c) -> p h c", c=CB)
        Tt = sb("T", [P, KW * 2 * CB])
        T = Tt[:, :].rearrange("p (k t c) -> p k t c", t=2, c=CB)
        ZT = Tt[:, 0:CB * P].rearrange("p (c s) -> p c s", s=P)
        landing = Tt[:, 0:H * CB].rearrange("p (h c) -> p h c", c=CB)
        O1 = [sb(f"O1_{i}", [CB + 1, 3, 4 * P]) for i in range(2)]
        comb = [sb(f"comb{i}", [CB, 4 * P]) for i in range(COMB_RING)]
        scratch = sb("scratch", [P, 24 * P])
        odd = [scratch[:, 4 * i * CB:4 * (i + 1) * CB].rearrange("p (h c) -> p h c", c=CB) for i in range(2)]
        rows_out = [St[:, (P + 8 * i) * CB:(P + 8 * i + 8) * CB].rearrange("p (h c) -> p h c", c=CB) for i in range(5)]
        rows_out += [scratch[:, 8 * (i + 1) * CB:8 * (i + 2) * CB].rearrange("p (h c) -> p h c", c=CB) for i in range(RING - 5)]
        mix_shared, mlp_shared = [[scratch[0:CB, (2 * m + i) * 4 * P:(2 * m + i + 1) * 4 * P] for i in range(2)]
                                  for m in range(2)]
        Yr = scratch[0:CB, 16 * P:20 * P]
        Yi = [scratch[0:CB, 20 * P:24 * P], sb("Yi1", [CB, 4 * P])[:, :]]

        def edge_parts(s):
            return [y[:, 2 * P:4 * P].rearrange("c (k s) -> c k s", s=P) for y in (Yr, Yi[s % 2])]

        w1_in = sb("w1_in", [CB, 2, CB])
        w2_in = sb("w2_in", [CB, 2, CB])
        b1_in = sb("b1_in", [CB, 2])
        scale_in = sb("scale_in", [P, 6])
        hw1_in = sb("hw1_in", [CB, CB])
        hw2_in = sb("hw2_in", [CB + 1, CB])
        hb1_in = sb("hb1_in", [CB, 1])
        M1 = [sb(f"M1_{i}", [CB, 3, CB]) for i in range(2)]
        M2 = [sb(f"M2_{i}", [CB + 1, 3, CB]) for i in range(2)]
        M1_next = sb("M1_next", [CB, 3, CB])
        M2_next = sb("M2_next", [CB + 1, 3, CB])
        bias1 = [sb(f"bias1_{i}", [CB, 2]) for i in range(2)]
        lam = [sb(f"lam{i}", [P, 2]) for i in range(2)]
        HM1 = sb("HM1", [CB, CB])
        HM2 = sb("HM2", [CB + 1, CB])
        hbias1 = sb("hbias1", [CB, 1])
        bank = ctx.enter_context(nc.psum_tensor("bank", [P, 8, 512], F32))

        const_loaded = sem("const_loaded")
        rows_loaded = [sem(f"rows_loaded{g}") for g in range(len(LOADS))]
        weights_loaded, hweights_loaded = sem("weights_loaded"), sem("hweights_loaded")
        w_ready, hw_ready = sem("w_ready"), sem("hw_ready")
        ones_set = sem("ones_set")
        x_ready = sem("x_ready")
        a_done, a_lower, a_taken = sem("a_done"), sem("a_lower"), sem("a_taken")
        b_done, b_taken = sem("b_done"), [sem("b_taken_act"), sem("b_taken_dve")]
        t_done, t_taken = sem("t_done"), [sem("t_taken_act"), sem("t_taken_dve")]
        c_done, c_taken = sem("c_done"), [sem("c_taken_act"), sem("c_taken_dve")]
        comb_ready = sem("comb_ready")
        mix_shared_done, mix_shared_ready = sem("mix_shared_done"), sem("mix_shared_ready")
        mlp_shared_done, mlp_shared_ready = sem("mlp_shared_done"), sem("mlp_shared_ready")
        mix_taken, relu_done, yr_ready = sem("mix_taken"), sem("relu_done"), sem("yr_ready")
        mlp_imaginary_done, yi_copied, yi_ready = sem("mlp_imaginary_done"), sem("yi_copied"), sem("yi_ready")
        next_ready = sem("next_ready")
        mix_done, o1_ready = sem("mix_done"), sem("o1_ready")
        mlp_done, upper_re, upper_im = sem("mlp_done"), sem("upper_re"), sem("upper_im")
        re_updated = sem("re_updated")
        s_updated = sem("s_updated")
        edge_step = sem("edge_step")
        d_done, odd_ready, rows_ready = sem("d_done"), sem("odd_ready"), sem("rows_ready")
        stored = [sem(f"stored{r}") for r in range(RING)]

        def mix_bank(s, t=0):
            return bank[0:CB, product(s, t) % 4, 0:GROUPS[s % N_G][1] * P]

        def mlp_bank(s, t=0):
            return bank[0:CB, 4 + product(s, t) % 4, 0:GROUPS[s % N_G][1] * P]

        def columns(s):
            return slice(0, GROUPS[s % N_G][1] * P)

        def a_bank(j):
            return bank[:, j % 4, 0:3 * 2 * KW]

        def b_bank(j):
            return bank[0:CB, 4 + j % 4, :]

        def b_cols(j):
            return slice(4 * j * P, min(4 * j + 4, 2 * KW) * P)

        def t_bank(j):
            return bank[:, j % 4, 0:4 * CB]

        def c_bank(j):
            return bank[:, 4 + j % 4, :]

        def d_banks(k):
            return [bank[:, (4, 6, 2)[k % 3] + t, :] for t in range(2)]

        def wait_for_stores(eng, u, j):
            if b_cols(j).stop > P * CB >= b_cols(j - 2 if j > 1 else j).stop:
                for ring in range(RING):
                    eng.wait_ge(stored[ring], u * STORES[ring] + 1)

        def take_b(copy, j, e):
            cols = b_cols(j)
            copy(Sflat[:, cols], b_bank(j)[:, 0:cols.stop - cols.start]).then_inc(b_taken[e], 1)

        def take_turn(copy, j, e):
            copy(ZT[:, :, 4 * j:4 * j + 4].rearrange("p c s -> p s c"),
                 t_bank(j).rearrange("p (s c) -> p s c", c=CB)).then_inc(t_taken[e], 1)

        def take_c(copy, j, e):
            copy(V[:, :, 4 * j:4 * j + 4].rearrange("p h c -> p c h"),
                 c_bank(j).rearrange("p (c h) -> p c h", h=P)).then_inc(c_taken[e], 1)

        def fold(eng, k, u, shared=False):
            if shared or k == LOAD_OF.index(LOAD_OF[k]):
                for g in (LOAD_OF[k] - 1, LOAD_OF[k]):
                    eng.wait_ge(rows_loaded[g], (u + 1) * 16)
            h0, n = 4 * k, min(4, NSUM - 4 * k)
            if n == 1 or k == 0:
                a = landing[:, h0, :]
                ins = eng.tensor_tensor(X[:, :, h0], a, a, ALU.add)
                if n == 1:
                    ins.then_inc(x_ready, 1)
                    return
                h0, n = 1, 3
            a = landing[:, h0:h0 + n, :]
            b = landing[:, H - h0 - n + 1:H - h0 + 1, :][:, ::-1, :]
            eng.tensor_tensor(X[:, :, h0:h0 + n].rearrange("p c s -> p s c"), a, b, ALU.add)
            eng.tensor_tensor(X[:, :, HALF + h0:HALF + h0 + n].rearrange("p c s -> p s c"), a, b,
                               ALU.subtract).then_inc(x_ready, 1)

        block = ctx.enter_context(nc.Block())

        @block.sync
        def _(sp):
            def load(g, image, chan):
                h0, n = LOADS[g]
                src = x[bass.ds(image, 1), h0:h0 + n, :, bass.ds(chan, CB)]
                sp.dma_start(landing[:, h0:h0 + n, :],
                             src.rearrange("a h w c -> w (a h) c")).then_inc(rows_loaded[g], 16)

            def load_weights(index, layer):
                sp.dma_start(w1_in[:, :, :], w1[bass.ds(index, 1)].rearrange("a c t o -> c (a t) o")).then_inc(weights_loaded, 16)
                sp.dma_start(w2_in[:, :, :], w2[bass.ds(index, 1)].rearrange("a c t o -> c (a t) o")).then_inc(weights_loaded, 16)
                sp.dma_start(M2_next[CB:CB + 1, 1:3, :], b2[bass.ds(index, 1)]).then_inc(weights_loaded, 16)
                sp.dma_start(b1_in[:, :], b1[bass.ds(index, 1)].rearrange("a c t -> c (a t)")).then_inc(weights_loaded, 16)
                sp.dma_start(scale_in[:, :], scales[layer]).then_inc(weights_loaded, 16)

            for g in range(len(LOADS)):
                load(g, 0, 0)
            sp.dma_start(const[:, :], consts).then_inc(const_loaded, 16)
            with sp.Fori(0, n_unit) as u:
                image, chan = sp.snap(u % n_img), sp.snap((u // n_img) * CB)
                following = sp.snap((u + 1) % n_unit)
                image1, chan1 = sp.snap(following % n_img), sp.snap((following // n_img) * CB)
                block_of = sp.snap(u // n_img)
                load_weights(block_of, 0)
                sp.wait_ge(w_ready, u * NLAYER + 1)
                load_weights(sp.snap(n_blk + block_of), 1)
                sp.wait_ge(b_done, u * N_B + N_B)
                for g in range(len(LOADS)):
                    load(g, image1, chan1)
                for layer in range(2, NLAYER):
                    sp.wait_ge(w_ready, u * NLAYER + layer)
                    load_weights(sp.snap(layer * n_blk + block_of), layer)
                sp.dma_start(hw1_in[:, :], hw1[bass.ds(block_of, 1)].rearrange("a c o -> c (a o)")).then_inc(hweights_loaded, 16)
                sp.dma_start(hw2_in[:, :], hw2[bass.ds(block_of, 1)].rearrange("a c o -> c (a o)")).then_inc(hweights_loaded, 16)
                sp.dma_start(hb1_in[:, :], hb1[bass.ds(block_of, 1)].rearrange("a c o -> c (a o)")).then_inc(hweights_loaded, 16)
                sp.wait_ge(w_ready, (u + 1) * NLAYER)
                sp.wait_ge(hw_ready, u + 1)
                for k in range(NCHUNK):
                    sp.wait_ge(rows_ready, u * NCHUNK + (k + 2))
                    for h0, n, at in chunk_rows(k):
                        dst = out[bass.ds(image, 1), h0:h0 + n, :, bass.ds(chan, CB)]
                        sp.dma_start(dst.rearrange("a h w c -> w (a h) c"),
                                     rows_out[k % RING][:, at:at + n, :]).then_inc(stored[k % RING], 16)
            for r in range(RING):
                sp.wait_ge(stored[r], 1 + n_unit * STORES[r])

        @block.gpsimd
        def _(pool):
            for k in range(0, NCHUNK, 2):
                fold(pool, k, 0, shared=True)
            def combine(u, s):
                p0, n = GROUPS[s % N_G]
                if s < N_G:
                    for e in range(2):
                        pool.wait_ge(b_taken[e], u * len(range(e, N_B, 2)) + b_groups(p0 + n - 1, e))
                else:
                    pool.wait_ge(s_updated, u * N_STEP + (s - N_G + 2))
                if s >= COMB_RING:
                    pool.wait_ge(mix_done, u * N_STEP + (s - COMB_RING + 1))
                pool.tensor_tensor(comb[s % COMB_RING][:, 0:n * P].rearrange("c (k s) -> c k s", s=P),
                                   S[:, p0:p0 + n, 0, :], S[:, p0:p0 + n, 1, :],
                                   ALU.add if s < N_COMPLEX else ALU.subtract).then_inc(comb_ready, 1)

            def sum_imaginary(u, s):
                pool.wait_ge(mlp_shared_ready, u * N_COMPLEX + (s + 1))
                pool.wait_ge(yi_copied, u * N_COMPLEX + (s + 1))
                y = Yi[s % 2][:, columns(s)]
                pool.tensor_tensor(y, y, mlp_shared[s % 2][:, columns(s)], ALU.add).then_inc(yi_ready, 1)

            def prepare_weights(u, layer, piece):
                it, b = u * NLAYER + layer, layer % 2
                if piece == 0:
                    pool.wait_ge(weights_loaded, (it + 1) * 80)
                if piece < 2:
                    nxt, w = ((M1_next, w1_in), (M2_next, w2_in))[piece]
                    pool.tensor_tensor(nxt[0:CB, 1, :], w[0:CB, 1, :], w[0:CB, 0, :], ALU.subtract)
                    pool.tensor_scalar(nxt[0:CB, 0, :], w[0:CB, 0, :], 1.0, None, ALU.mult)
                    pool.tensor_tensor(nxt[0:CB, 2, :], w[0:CB, 0, :], w[0:CB, 1, :], ALU.add).then_inc(next_ready, 1)
                if piece == 2:
                    pool.wait_ge(next_ready, (it + 1) * 2)
                    if layer:
                        pool.wait_ge(s_updated, u * N_STEP + (layer - 1) * N_G + 1)
                    scale_weights(M1[b], M1_next, 0)
                if piece == 3:
                    scale_weights(M2[b], M2_next, 2)
                    pool.tensor_copy(bias1[b][:, :], b1_in[:, :])
                    pool.tensor_copy(lam[b][:, :], scale_in[:, 4:6]).then_inc(w_ready, 1)

            def scale_weights(m, nxt, column):
                rows = m.shape[0]
                pool.tensor_tensor(m[:, 0:2, :].rearrange("c t o -> c (t o)"), nxt[:, 0:2, :].rearrange("c t o -> c (t o)"),
                                   scale_in[0:rows, column:column + 1].to_broadcast([rows, 2 * CB]), ALU.mult)
                return pool.tensor_tensor(m[:, 2, :], nxt[:, 2, :],
                                          scale_in[0:rows, column + 1:column + 2].to_broadcast([rows, CB]), ALU.mult)

            pool.wait_ge(const_loaded, 16)
            pool.wait_ge(ones_set, 3)
            with pool.Fori(0, n_unit) as u:
                for piece in range(4):
                    prepare_weights(u, 0, piece)
                for ahead in range(2):
                    combine(u, ahead)
                for s in range(N_COMPLEX):
                    layer, i = divmod(s, N_G)
                    pool.wait_ge(relu_done, u * N_COMPLEX + (s + 1))
                    o = O1[s % 2]
                    pool.tensor_tensor(o[0:CB, 2, columns(s)], o[0:CB, 0, columns(s)], o[0:CB, 1, columns(s)],
                                       ALU.add).then_inc(o1_ready, 1)
                    if s >= 1:
                        sum_imaginary(u, s - 1)
                    combine(u, s + 2)
                    k, between = divmod(s - N_G, 2)
                    if k >= 0 and not between:
                        fold(pool, k, u + 1)
                    if layer + 1 < NLAYER and i in PREPARE_AT:
                        prepare_weights(u, layer + 1, PREPARE_AT.index(i))
                    if layer + 1 == NLAYER and i == PREPARE_AT[0] + 1:
                        pool.wait_ge(hweights_loaded, (u + 1) * 48)
                        pool.tensor_tensor(HM1[:, :], hw1_in[:, :], mat["hartley_scale"][0:CB].to_broadcast([CB, CB]), ALU.mult)
                        pool.tensor_copy(hbias1[:, :], hb1_in[:, :])
                        pool.tensor_scalar(HM2[:, :], hw2_in[:, :], HARTLEY_GAIN, None, ALU.mult).then_inc(hw_ready, 1)
                sum_imaginary(u, N_COMPLEX - 1)
                for s in range(N_COMPLEX + 2, N_STEP):
                    combine(u, s)
                pool.wait_ge(mlp_done, u * N_STEP + N_STEP)

        @block.tensor
        def _(pe):
            mm = pe.matmul

            def forward(u):
                pe.wait_ge(x_ready, (u + 1) * NCHUNK)
                for j in range(N_A):
                    if j >= 4:
                        pe.wait_ge(a_taken, u * N_A + (j - 3))
                    for i in range(3):
                        last = mm(a_bank(j)[:, i * 2 * KW:(i + 1) * 2 * KW], X[:, 3 * j + i, :], mat["dft_w"],
                                  start=True, stop=True)
                    last.then_inc(a_done, 1)
                pe.wait_ge(rows_ready, u * NCHUNK + 1)
                pe.wait_ge(a_taken, u * N_A + N_A)
                for j in range(N_B):
                    if j >= 4:
                        pe.wait_ge(b_taken[j % 2], u * len(range(j % 2, N_B, 2)) + ((j - 4) // 2 + 1))
                    for q in range(4 * j, min(4 * j + 4, 2 * KW)):
                        i = q - 4 * j
                        last = mm(b_bank(j)[:, i * P:(i + 1) * P], T[:, q // 2, q % 2, :],
                                  mat[("dft_h_re", "dft_h_im")[q % 2]], start=True, stop=True)
                    last.then_inc(b_done, 1)

            def wait_for_bank(u, s, t, waited, complex_taken, taken, taken_base):
                b = step_before(s, t)
                if b is None or b in waited:
                    return
                waited.add(b)
                if b < N_COMPLEX:
                    for reader in complex_taken:
                        pe.wait_ge(reader, u * N_COMPLEX + (b + 1))
                else:
                    pe.wait_ge(taken, u * N_STEP + (b + 1 + taken_base))

            def layers(u):
                mix_waited, mlp_waited = set(), set()
                for s in range(N_STEP + 1):
                    if s < N_STEP:
                        b = s // N_G % 2
                        if s % N_G == 0:
                            if s < N_COMPLEX:
                                pe.wait_ge(w_ready, u * NLAYER + (s // N_G + 1))
                            else:
                                pe.wait_ge(hw_ready, u + 1)
                        pe.wait_ge(comb_ready, u * N_STEP + (s + 1))
                        v = comb[s % COMB_RING][:, columns(s)]
                        wait_for_bank(u, s, 0, mix_waited, [mix_taken], o1_ready, 0)
                        if s < N_COMPLEX:
                            p0, n = GROUPS[s % N_G]
                            mm(mix_bank(s), M1[b][:, 0, :], v, start=True, stop=True).then_inc(mix_shared_done, 1)
                            for t in (1, 2):
                                wait_for_bank(u, s, t, mix_waited, [mix_taken], o1_ready, 0)
                                last = mm(mix_bank(s, t).rearrange("c (k s) -> c k s", s=P), M1[b][:, t, :],
                                          S[:, p0:p0 + n, t - 1, :], start=True, stop=True)
                        else:
                            last = mm(mix_bank(s), HM1[:, :], v, start=True, stop=True)
                        last.then_inc(mix_done, 1)
                    if s >= 1:
                        j = s - 1
                        b = j // N_G % 2
                        o1 = O1[j % 2]
                        pe.wait_ge(o1_ready, u * N_STEP + (j + 1))
                        wait_for_bank(u, j, 0, mlp_waited, [yi_copied, yr_ready], s_updated, 1)
                        if j < N_COMPLEX:
                            mm(mlp_bank(j), M2[b][0:CB, 0, :], o1[0:CB, 2, columns(j)], start=True,
                               stop=True).then_inc(mlp_shared_done, 1)
                            for t in (1, 2):
                                wait_for_bank(u, j, t, mlp_waited, [yi_copied, yr_ready], s_updated, 1)
                                last = mm(mlp_bank(j, t), M2[b][:, t, :], o1[:, t - 1, columns(j)], start=True, stop=True)
                                if t == 1:
                                    last.then_inc(mlp_imaginary_done, 1)
                        else:
                            last = mm(mlp_bank(j), HM2[:, :], o1[:, 0, columns(j)], start=True, stop=True)
                        last.then_inc(mlp_done, 1)

            def inverse(u):
                for j in range(N_T):
                    slots = range(4 * j, 4 * j + 4)
                    pe.wait_ge(s_updated, u * N_STEP + (N_COMPLEX + 2 + max(group_of(s if s < KW else s - KW + 2) for s in slots)))
                    if j >= 4:
                        pe.wait_ge(t_taken[j % 2], u * (N_T // 2) + ((j - 4) // 2 + 1))
                    for i, s in enumerate(slots):
                        o = t_bank(j)[:, i * CB:(i + 1) * CB]
                        pos, part = (s, 0) if s < KW else (s - KW + 2, 1)
                        last = mm(o, S[:, pos, part, :], mat["identity"][0:CB, :], start=True, stop=s >= 2)
                        if s < 2:
                            last = mm(o, S[:, pos, 1, :], mat["identity"][0:CB, :], start=False, stop=True)
                    last.then_inc(t_done, 1)
                for e in range(2):
                    pe.wait_ge(t_taken[e], (u + 1) * (N_T // 2))
                for j in range(N_C):
                    if j >= 4:
                        pe.wait_ge(c_taken[j % 2], u * (N_C // 2) + ((j - 4) // 2 + 1))
                    for i in range(4):
                        last = mm(c_bank(j)[:, i * P:(i + 1) * P], ZT[:, 4 * j + i, :], mat["idft_h"],
                                  start=True, stop=True)
                    last.then_inc(c_done, 1)
                for e in range(2):
                    pe.wait_ge(c_taken[e], (u + 1) * (N_C // 2))
                for k in range(NCHUNK):
                    if k >= 3:
                        pe.wait_ge(rows_ready, u * NCHUNK + (k - 1))
                    even, odds = d_banks(k)
                    h0, n = 4 * k, min(4, NSUM - 4 * k)
                    s = 1 if n == 1 or k == 0 else 0
                    if n > s:
                        mm(odds[:, s * CB:n * CB], mat["idft_w_diff"], V[:, HALF + h0 + s:HALF + h0 + n, :],
                           start=True, stop=True)
                    mm(even[:, 0:n * CB], mat["idft_w_sum"], V[:, h0:h0 + n, :], start=True,
                       stop=True).then_inc(d_done, 1)
                pe.wait_ge(rows_ready, u * NCHUNK + (2 + max(k for k in range(NCHUNK) if k % 3 == 2)))

            pe.wait_ge(const_loaded, 16)
            with pe.Fori(0, n_unit) as u:
                forward(u)
                layers(u)
                inverse(u)

        @block.scalar
        def _(act):
            def copy(o, i):
                return act.activation(o, i, ACT.Copy)

            def layers(u):
                for s in range(N_COMPLEX + 1):
                    c = u * N_COMPLEX + s
                    if s < N_COMPLEX:
                        act.wait_ge(mix_shared_done, c + 1)
                        if s >= 2:
                            act.wait_ge(mix_taken, c - 1)
                        copy(mix_shared[s % 2][:, columns(s)], mix_bank(s)).then_inc(mix_shared_ready, 1)
                    if s >= 1:
                        j = s - 1
                        act.wait_ge(mlp_shared_done, c)
                        if j >= 2:
                            act.wait_ge(yr_ready, c - 2)
                            act.wait_ge(yi_ready, c - 2)
                        copy(mlp_shared[j % 2][:, columns(j)], mlp_bank(j)).then_inc(mlp_shared_ready, 1)
                    if s < N_COMPLEX:
                        b = s // N_G % 2
                        if s % N_G == 0:
                            act.wait_ge(w_ready, u * NLAYER + (s // N_G + 1))
                        act.wait_ge(mix_taken, c + 1)
                        for t in range(2):
                            o = O1[s % 2][0:CB, t, columns(s)]
                            last = act.activation(o, o, ACT.Relu, bias=bias1[b][:, t:t + 1])
                        last.then_inc(relu_done, 1)
                    if s >= 1:
                        act.wait_ge(mlp_imaginary_done, c)
                        if j >= 2:
                            act.wait_ge(s_updated, u * N_STEP + j)
                        copy(Yi[j % 2][:, columns(j)], mlp_bank(j, 1)).then_inc(yi_copied, 1)
                act.wait_ge(hw_ready, u + 1)
                for s in range(N_COMPLEX, N_STEP):
                    act.wait_ge(mix_done, u * N_STEP + (s + 1))
                    act.wait_ge(mlp_done, u * N_STEP + (s - 1))
                    act.activation(O1[s % 2][0:CB, 0, columns(s)], mix_bank(s), ACT.Relu,
                                   bias=hbias1[:, 0:1]).then_inc(o1_ready, 1)

            with act.Fori(0, n_unit) as u:
                for j in range(N_A):
                    act.wait_ge(a_lower, u * N_A + (j + 1))
                    copy(T[0:NSUM, :, :, 3 * j:3 * j + 3].rearrange("p k t c -> p c t k"),
                         a_bank(j)[0:NSUM].rearrange("p (c t k) -> p c t k", t=2, k=KW)).then_inc(a_taken, 1)
                for j in range(0, N_B, 2):
                    wait_for_stores(act, u, j)
                    act.wait_ge(b_done, u * N_B + (j + 1))
                    take_b(copy, j, 0)
                layers(u)
                act.wait_ge(x_ready, (u + 2) * NCHUNK)
                for j in range(0, N_T, 2):
                    act.wait_ge(t_done, u * N_T + (j + 1))
                    take_turn(copy, j, 0)
                for j in range(0, N_C, 2):
                    act.wait_ge(c_done, u * N_C + (j + 1))
                    take_c(copy, j, 0)
                for k in range(NCHUNK - 1):
                    act.wait_ge(d_done, u * NCHUNK + (k + 1))
                    if k >= 2:
                        act.wait_ge(rows_ready, u * NCHUNK + k)
                    s = 1 if k == 0 else 0
                    copy(odd[k % 2][:, s:4, :], d_banks(k)[1][:, s * CB:4 * CB].rearrange("p (h c) -> p h c", c=CB)).then_inc(odd_ready, 1)

        @block.vector
        def _(dve):
            for i in range(2):
                dve.memset(O1[i][CB:CB + 1, :, :], 1.0).then_inc(ones_set, 1)
            dve.memset(M2_next[CB:CB + 1, 0, :], 0.0).then_inc(ones_set, 1)
            dve.wait_ge(ones_set, 3)
            dve.memset(Yi[1][:, 0:2 * P], 0.0).then_inc(s_updated, 1)
            dve.memset(Yi[1][:, 2 * P:4 * P], 0.0).then_inc(rows_ready, 1)
            for r in range(RING):
                dve.memset(rows_out[r][:, :, :], 0.0).then_inc(stored[r], 1)

            def add_shrunk(u, s, t, y, hi, lo, signal):
                p0, n = GROUPS[s % N_G]
                v = S[:, p0:p0 + n, t, :]
                y = y.rearrange("c (k s) -> c k s", s=P)
                upper, steps = (upper_im, N_COMPLEX) if t else (upper_re, N_STEP)
                dve.scalar_tensor_tensor(v, y, hi, v, ALU.max, ALU.add).then_inc(upper, 1)
                dve.wait_ge(upper, u * plain(steps - 1) + plain(s))
                dve.scalar_tensor_tensor(v, y, lo, v, ALU.min, ALU.add).then_inc(signal, 1)

            def add_edges(u, s, y, hi, lo, factor):
                parts = len(y)
                edge = edge_parts(s)
                y = [part.rearrange("c (k s) -> c k s", s=P) for part in y]
                e0 = u * (4 * (NLAYER + 1)) + 4 * (s // N_G)
                for t in range(parts):
                    last = dve.tensor_scalar(edge[t], y[t], hi, None, ALU.max)
                last.then_inc(edge_step, 1)
                dve.wait_ge(edge_step, e0 + 1)
                for t in range(parts):
                    last = dve.scalar_tensor_tensor(edge[t], y[t], lo, edge[t], ALU.min, ALU.add)
                last.then_inc(edge_step, 1)
                dve.wait_ge(edge_step, e0 + 2)
                for t in range(parts):
                    v = S[:, 0:2, t, :]
                    last = dve.scalar_tensor_tensor(v, edge[t], factor, v, ALU.mult, ALU.add)
                last.then_inc(edge_step, 1)
                dve.wait_ge(edge_step, e0 + 3)
                for t in range(parts):
                    f = factor if t == 0 else -factor
                    v = S[:, 0:2, t, :]
                    dve.scalar_tensor_tensor(v[:, :, 0:1], edge[t][:, :, 0:1], f, v[:, :, 0:1], ALU.mult, ALU.add)
                    last = dve.scalar_tensor_tensor(v[:, :, 1:P], edge[t][:, :, 1:P][:, :, ::-1], f, v[:, :, 1:P],
                                                    ALU.mult, ALU.add)
                last.then_inc(edge_step, 1)
                dve.wait_ge(edge_step, e0 + 4)
                if parts == 2:
                    dve.memset(edge[1][:, 0, 0:1], 0.0).then_inc(re_updated, 1)
                dve.memset(edge[0][:, 0, 0:1], 0.0).then_inc(s_updated, 1)

            def layers(u):
                for s in range(N_STEP + 1):
                    c, g = u * N_COMPLEX + s, u * N_STEP + s
                    if s < N_COMPLEX:
                        dve.wait_ge(mix_shared_ready, c + 1)
                        if s >= 2:
                            dve.wait_ge(mlp_done, g - 1)
                        dve.wait_ge(mix_done, g + 1)
                        for t, own in ((1, 1), (0, 2)):
                            last = dve.tensor_tensor(O1[s % 2][0:CB, t, columns(s)], mix_bank(s, own),
                                                     mix_shared[s % 2][:, columns(s)], ALU.add)
                        last.then_inc(mix_taken, 1)
                    j = s - 2
                    if 0 <= j < N_COMPLEX:
                        hi, lo = [lam[j // N_G % 2][0:CB, i:i + 1] for i in range(2)]
                        dve.wait_ge(yi_ready, c - 1)
                        if j % N_G == EDGES:
                            add_edges(u, j, [Yr[:, columns(j)], Yi[j % 2][:, columns(j)]], hi, lo, 0.5)
                        else:
                            add_shrunk(u, j, 1, Yi[j % 2][:, columns(j)], hi, lo, s_updated)
                    j = s - 1
                    if 0 <= j < N_COMPLEX:
                        dve.wait_ge(mlp_shared_ready, c)
                        dve.wait_ge(mlp_done, g)
                        if j >= 1:
                            dve.wait_ge(re_updated, c - 1)
                            if (j - 1) % N_G == EDGES:
                                dve.wait_ge(s_updated, g)
                        dve.tensor_tensor(Yr[:, columns(j)], mlp_bank(j, 2), mlp_shared[j % 2][:, columns(j)],
                                          ALU.add).then_inc(yr_ready, 1)
                        if j % N_G == 0:
                            dve.wait_ge(w_ready, u * NLAYER + (j // N_G + 1))
                        dve.wait_ge(yr_ready, c)
                        if j % N_G != EDGES:
                            hi, lo = [lam[j // N_G % 2][0:CB, i:i + 1] for i in range(2)]
                            add_shrunk(u, j, 0, Yr[:, columns(j)], hi, lo, re_updated)
                    elif j >= N_COMPLEX:
                        dve.wait_ge(mlp_done, g)
                        limit = LAMBDA * HARTLEY_GAIN
                        if j % N_G == EDGES:
                            add_edges(u, j, [mlp_bank(j)], limit, -limit, 1.0)
                        else:
                            add_shrunk(u, j, 0, mlp_bank(j), limit, -limit, s_updated)

            for k in range(1, NCHUNK, 2):
                fold(dve, k, 0, shared=True)
            with dve.Fori(0, n_unit) as u:
                for j in range(N_A):
                    dve.wait_ge(a_done, u * N_A + (j + 1))
                    dve.tensor_copy(T[HALF:P, :, :, 3 * j:3 * j + 3].rearrange("p k t c -> p c t k"),
                                    a_bank(j)[HALF:P].rearrange("p (c t k) -> p c t k", t=2, k=KW)[:, :, ::-1, :]).then_inc(a_lower, 1)
                for j in range(1, N_B, 2):
                    wait_for_stores(dve, u, j)
                    dve.wait_ge(b_done, u * N_B + (j + 1))
                    take_b(dve.tensor_copy, j, 1)
                layers(u)
                dve.wait_ge(x_ready, (u + 2) * NCHUNK)
                for j in range(1, N_T, 2):
                    dve.wait_ge(t_done, u * N_T + (j + 1))
                    take_turn(dve.tensor_copy, j, 1)
                for j in range(1, N_C, 2):
                    dve.wait_ge(c_done, u * N_C + (j + 1))
                    take_c(dve.tensor_copy, j, 1)
                for k in range(NCHUNK):
                    if k < NCHUNK - 1:
                        dve.wait_ge(odd_ready, u * (NCHUNK - 1) + (k + 1))
                    else:
                        dve.wait_ge(d_done, u * NCHUNK + NCHUNK)
                    dve.wait_ge(stored[k % RING], u * STORES[k % RING] + (1 + STORES_BEFORE[k]))
                    n = min(4, NSUM - 4 * k)
                    s = 1 if n == 1 or k == 0 else 0
                    even = d_banks(k)[0][:, 0:n * CB].rearrange("p (h c) -> p h c", c=CB)
                    o = rows_out[k % RING]
                    if s:
                        last = dve.tensor_copy(o[:, 0, :], even[:, 0, :])
                    if n > s:
                        dve.tensor_tensor(o[:, s:n, :], even[:, s:n, :], odd[k % 2][:, s:n, :], ALU.add)
                        last = dve.tensor_tensor(o[:, 4:4 + n - s, :][:, ::-1, :], even[:, s:n, :], odd[k % 2][:, s:n, :],
                                                 ALU.subtract)
                    last.then_inc(rows_ready, 1)


def build(nc, arrays, shape):
    ins = {}
    for name, a in arrays.items():
        ins[name] = nc.dram_tensor(name, a.shape, F32, kind="ExternalInput").ap()
    out = nc.dram_tensor("out", shape, F32, kind="ExternalOutput").ap()
    spectral_layers(nc, ins["x"], ins["w1"], ins["w2"], ins["b1"], ins["b2"], ins["scales"], ins["hw1"], ins["hw2"],
                    ins["hb1"], ins["consts"], out, shape[0], shape[3] // CB)


def lay_out(x, ws):
    c = np.ascontiguousarray
    w1 = np.stack([ws[f"L{n}_conv_w1"] for n in range(NLAYER)])
    w2 = np.stack([ws[f"L{n}_conv_w2"] for n in range(NLAYER)])
    b1 = np.stack([ws[f"L{n}_conv_b1"] for n in range(NLAYER)])
    b2 = np.stack([ws[f"L{n}_conv_b2"] for n in range(NLAYER)])
    hw2 = np.concatenate([ws["L3_conv_w2"][0], ws["L3_conv_b2"][0][:, None, :]], axis=1)
    n = NLAYER * w1.shape[2]
    return {
        "x": c(x),
        "w1": c(w1.transpose(0, 2, 3, 1, 4)).reshape(n, CB, 2, CB),
        "w2": c(w2.transpose(0, 2, 3, 1, 4)).reshape(n, CB, 2, CB),
        "b1": c(b1.transpose(0, 2, 3, 1)).reshape(n, CB, 2),
        "b2": c(b2[:, ::-1].transpose(0, 2, 1, 3)).reshape(n, 1, 2, CB),
        "scales": layer_scales(),
        "hw1": c(ws["L3_conv_w1"][0]),
        "hw2": c(hw2),
        "hb1": c(ws["L3_conv_b1"][0][:, :, None]),
        "consts": constants(),
    }


def kernel(**inputs):
    import concourse.bacc as _bacc
    from concourse.bass_utils import run_bass_kernel_spmd as _run

    ws = {k: np.asarray(v) for k, v in inputs.items() if k != "x"}
    arrays = lay_out(np.asarray(inputs["x"]), ws)
    nc = _bacc.Bacc("TRN2", target_bir_lowering=False, num_devices=1)
    build(nc, arrays, arrays["x"].shape)
    r = _run(nc, [arrays], core_ids=[0])
    return r.results[0]["out"]
```
